# Optimizing a Trainium2 kernel written in Bass

```python
import numpy as np
import jax
import jax.numpy as jnp

def _softmax(x, axis=-1):
    return jax.nn.softmax(x, axis=axis)

def _gelu(x):
    return jax.nn.gelu(x, approximate=True)

def _silu(x):
    return jax.nn.silu(x)

def _sigmoid(x):
    return jax.nn.sigmoid(x)

def _layernorm(x, axis=-1, eps=1e-05):
    m = jnp.mean(x, axis=axis, keepdims=True)
    v = jnp.var(x, axis=axis, keepdims=True)
    return (x - m) / jnp.sqrt(v + eps)

def _scatter_add(tgt, idx, src, axis=0):
    return tgt.at[idx].add(src)

def _segment_sum(src, seg, n):
    return jax.ops.segment_sum(src, seg, n)
kernel_name = 'mk_xattn_seq_d2_seqx_r8_3f2e01'

def setup_inputs(seed: int=0):
    np.random.seed(seed)
    _w = jnp.asarray

    def _rec_inputs():
        import jax
        import jax.numpy as jnp
        _rk = jax.random.key(seed)
        x = -0.0002928 + 1 * jax.random.normal(jax.random.fold_in(_rk, 1), (4, 256, 128), jnp.float32)
        _lenS = 256 - jax.random.randint(jax.random.fold_in(_rk, 7), (4,), 0, max(1, 256 // 4) + 1, jnp.int32)
        _lenS2 = 256 - jax.random.randint(jax.random.fold_in(_rk, 8), (4,), 0, max(1, 256 // 4) + 1, jnp.int32)
        _ctx_768P = jax.random.normal(jax.random.fold_in(_rk, 11), (4, 16, 96), jnp.float32)
        _ctx_768c = jax.random.dirichlet(jax.random.fold_in(_rk, 511), 0.3 * jnp.ones((16,), jnp.float32), (4, 256))
        _ctx_768t = jnp.einsum('bsk,bkd->bsd', _ctx_768c, _ctx_768P)
        _ctx_768t = _ctx_768t * jax.lax.rsqrt(jnp.mean(jnp.square(_ctx_768t)) + 1e-12) * 0.953939
        ctx_768 = -0.00423632 + 0.9977 * (_ctx_768t + 0.3 * jax.random.normal(jax.random.fold_in(_rk, 611), (4, 256, 96), jnp.float32))
        return (x, ctx_768)
    x, ctx_768 = _rec_inputs()

    def _L0_xattn_setup():
        import jax, jax.numpy as jnp
        import numpy as np
        DIM, HEADS, DHEAD, CTX_DIM = (128, 16, 64, 96)
        INNER = HEADS * DHEAD
        FF_HID = 4 * DIM
        EPS = 1e-05

        def _ln(x, g, b):
            mu = jnp.mean(x, axis=-1, keepdims=True)
            var = jnp.mean(jnp.square(x - mu), axis=-1, keepdims=True)
            return (x - mu) * jax.lax.rsqrt(var + EPS) * g + b

        def _attn(x, ctx, Wq, Wk, Wv, Wo, bo):
            b, n, _ = x.shape
            m = ctx.shape[1]
            q = (x @ Wq).reshape(b, n, HEADS, DHEAD)
            k = (ctx @ Wk).reshape(b, m, HEADS, DHEAD)
            v = (ctx @ Wv).reshape(b, m, HEADS, DHEAD)
            scale = DHEAD ** (-0.5)
            sim = jnp.einsum('bihd,bjhd->bhij', q, k) * scale
            attn = jax.nn.softmax(sim, axis=-1)
            out = jnp.einsum('bhij,bjhd->bihd', attn, v).reshape(b, n, INNER)
            return out @ Wo + bo
        key = jax.random.key(seed)
        ks = jax.random.split(key, 24)

        def w(k, shape, fan_in):
            return jax.random.normal(k, shape, jnp.float32) * fan_in ** (-0.5)
        inp = {'x': jax.random.normal(ks[0], (2, 256, DIM), jnp.float32), 'context': jax.random.normal(ks[1], (2, 77, CTX_DIM), jnp.float32), 'Wq1': w(ks[2], (DIM, INNER), DIM), 'Wk1': w(ks[3], (DIM, INNER), DIM), 'Wv1': w(ks[4], (DIM, INNER), DIM), 'Wo1': w(ks[5], (INNER, DIM), INNER), 'bo1': jnp.zeros((DIM,), jnp.float32), 'Wq2': w(ks[6], (DIM, INNER), DIM), 'Wk2': w(ks[7], (CTX_DIM, INNER), CTX_DIM), 'Wv2': w(ks[8], (CTX_DIM, INNER), CTX_DIM), 'Wo2': w(ks[9], (INNER, DIM), INNER), 'bo2': jnp.zeros((DIM,), jnp.float32), 'Wp': w(ks[10], (DIM, 2 * FF_HID), DIM), 'bp': jnp.zeros((2 * FF_HID,), jnp.float32), 'W2': w(ks[11], (FF_HID, DIM), FF_HID), 'b2': jnp.zeros((DIM,), jnp.float32), 'g1': jnp.ones((DIM,), jnp.float32), 'be1': jnp.zeros((DIM,), jnp.float32), 'g2': jnp.ones((DIM,), jnp.float32), 'be2': jnp.zeros((DIM,), jnp.float32), 'g3': jnp.ones((DIM,), jnp.float32), 'be3': jnp.zeros((DIM,), jnp.float32)}
        return inp
    _L0_xattn_all = _L0_xattn_setup()
    _L0_xattn_in = {k: v for k, v in _L0_xattn_all.items() if k in ('Wq1', 'Wk1', 'Wv1', 'Wo1', 'bo1', 'Wq2', 'Wk2', 'Wv2', 'Wo2', 'bo2', 'Wp', 'bp', 'W2', 'b2', 'g1', 'be1', 'g2', 'be2', 'g3', 'be3')}
    del _L0_xattn_all

    def _L1_xattn_setup():
        import jax, jax.numpy as jnp
        import numpy as np
        B, N, D, H, M, CD = (2, 256, 128, 16, 77, 96)
        DH = D // H
        FF = 4 * D
        NBITS = 8
        EPS = 1e-05

        def fake_quant_w(w, n_bits=NBITS):
            levels = 2 ** n_bits - 1
            mn = jnp.min(w)
            mx = jnp.max(w)
            delta = (mx - mn) / levels
            zp = jnp.round(-mn / delta)
            wq = jnp.clip(jnp.round(w / delta) + zp, 0, levels)
            wdq = (wq - zp) * delta
            return w + jax.lax.stop_gradient(wdq - w)

        def layernorm(x, g, b):
            mu = jnp.mean(x, axis=-1, keepdims=True)
            var = jnp.mean((x - mu) ** 2, axis=-1, keepdims=True)
            return (x - mu) * jax.lax.rsqrt(var + EPS) * g + b

        def linear(x, w, b=None):
            y = x @ fake_quant_w(w).T
            return y if b is None else y + b

        def cross_attn(x, ctx, qw, kw, vw, ow, ob):
            Bq, Nq, _ = x.shape
            Nk = ctx.shape[1]
            q = linear(x, qw).reshape(Bq, Nq, H, DH)
            k = linear(ctx, kw).reshape(Bq, Nk, H, DH)
            v = linear(ctx, vw).reshape(Bq, Nk, H, DH)
            scale = DH ** (-0.5)
            sim = jnp.einsum('bihd,bjhd->bhij', q, k) * scale
            attn = jax.nn.softmax(sim, axis=-1)
            out = jnp.einsum('bhij,bjhd->bihd', attn, v).reshape(Bq, Nq, D)
            return linear(out, ow, ob)

        def geglu_ff(x, w1, b1, w2, b2):
            h = linear(x, w1, b1)
            hidden, gate = jnp.split(h, 2, axis=-1)
            return linear(hidden * jax.nn.gelu(gate), w2, b2)
        key = jax.random.key(seed)
        ks = jax.random.split(key, 24)
        W = lambda k, o, i: jax.random.normal(k, (o, i), jnp.float32) * 0.02
        return {'x': jax.random.normal(ks[0], (B, N, D), jnp.float32), 'context': jax.random.normal(ks[1], (B, M, CD), jnp.float32), 'ln1_g': 1.0 + 0.1 * jax.random.normal(ks[2], (D,), jnp.float32), 'ln1_b': 0.1 * jax.random.normal(ks[3], (D,), jnp.float32), 'ln2_g': 1.0 + 0.1 * jax.random.normal(ks[4], (D,), jnp.float32), 'ln2_b': 0.1 * jax.random.normal(ks[5], (D,), jnp.float32), 'ln3_g': 1.0 + 0.1 * jax.random.normal(ks[6], (D,), jnp.float32), 'ln3_b': 0.1 * jax.random.normal(ks[7], (D,), jnp.float32), 'q1_w': W(ks[8], D, D), 'k1_w': W(ks[9], D, D), 'v1_w': W(ks[10], D, D), 'o1_w': W(ks[11], D, D), 'o1_b': jnp.zeros((D,), jnp.float32), 'q2_w': W(ks[12], D, D), 'k2_w': W(ks[13], D, CD), 'v2_w': W(ks[14], D, CD), 'o2_w': W(ks[15], D, D), 'o2_b': jnp.zeros((D,), jnp.float32), 'ff1_w': W(ks[16], 2 * FF, D), 'ff1_b': jnp.zeros((2 * FF,), jnp.float32), 'ff2_w': W(ks[17], D, FF), 'ff2_b': jnp.zeros((D,), jnp.float32)}
    _L1_xattn_all = _L1_xattn_setup()
    _L1_xattn_in = {k: v for k, v in _L1_xattn_all.items() if k in ('ln1_g', 'ln1_b', 'ln2_g', 'ln2_b', 'ln3_g', 'ln3_b', 'q1_w', 'k1_w', 'v1_w', 'o1_w', 'o1_b', 'q2_w', 'k2_w', 'v2_w', 'o2_w', 'o2_b', 'ff1_w', 'ff1_b', 'ff2_w', 'ff2_b')}
    del _L1_xattn_all
    return {'x': x, 'ctx_768': ctx_768, 'L0_xattn_Wq1': _L0_xattn_in['Wq1'], 'L0_xattn_Wk1': _L0_xattn_in['Wk1'], 'L0_xattn_Wv1': _L0_xattn_in['Wv1'], 'L0_xattn_Wo1': _L0_xattn_in['Wo1'], 'L0_xattn_bo1': _L0_xattn_in['bo1'], 'L0_xattn_Wq2': _L0_xattn_in['Wq2'], 'L0_xattn_Wk2': _L0_xattn_in['Wk2'], 'L0_xattn_Wv2': _L0_xattn_in['Wv2'], 'L0_xattn_Wo2': _L0_xattn_in['Wo2'], 'L0_xattn_bo2': _L0_xattn_in['bo2'], 'L0_xattn_Wp': _L0_xattn_in['Wp'], 'L0_xattn_bp': _L0_xattn_in['bp'], 'L0_xattn_W2': _L0_xattn_in['W2'], 'L0_xattn_b2': _L0_xattn_in['b2'], 'L0_xattn_g1': _L0_xattn_in['g1'], 'L0_xattn_be1': _L0_xattn_in['be1'], 'L0_xattn_g2': _L0_xattn_in['g2'], 'L0_xattn_be2': _L0_xattn_in['be2'], 'L0_xattn_g3': _L0_xattn_in['g3'], 'L0_xattn_be3': _L0_xattn_in['be3'], 'L1_xattn_ln1_g': _L1_xattn_in['ln1_g'], 'L1_xattn_ln1_b': _L1_xattn_in['ln1_b'], 'L1_xattn_ln2_g': _L1_xattn_in['ln2_g'], 'L1_xattn_ln2_b': _L1_xattn_in['ln2_b'], 'L1_xattn_ln3_g': _L1_xattn_in['ln3_g'], 'L1_xattn_ln3_b': _L1_xattn_in['ln3_b'], 'L1_xattn_q1_w': _L1_xattn_in['q1_w'], 'L1_xattn_k1_w': _L1_xattn_in['k1_w'], 'L1_xattn_v1_w': _L1_xattn_in['v1_w'], 'L1_xattn_o1_w': _L1_xattn_in['o1_w'], 'L1_xattn_o1_b': _L1_xattn_in['o1_b'], 'L1_xattn_q2_w': _L1_xattn_in['q2_w'], 'L1_xattn_k2_w': _L1_xattn_in['k2_w'], 'L1_xattn_v2_w': _L1_xattn_in['v2_w'], 'L1_xattn_o2_w': _L1_xattn_in['o2_w'], 'L1_xattn_o2_b': _L1_xattn_in['o2_b'], 'L1_xattn_ff1_w': _L1_xattn_in['ff1_w'], 'L1_xattn_ff1_b': _L1_xattn_in['ff1_b'], 'L1_xattn_ff2_w': _L1_xattn_in['ff2_w'], 'L1_xattn_ff2_b': _L1_xattn_in['ff2_b']}

def reference(x, ctx_768, L0_xattn_Wq1, L0_xattn_Wk1, L0_xattn_Wv1, L0_xattn_Wo1, L0_xattn_bo1, L0_xattn_Wq2, L0_xattn_Wk2, L0_xattn_Wv2, L0_xattn_Wo2, L0_xattn_bo2, L0_xattn_Wp, L0_xattn_bp, L0_xattn_W2, L0_xattn_b2, L0_xattn_g1, L0_xattn_be1, L0_xattn_g2, L0_xattn_be2, L0_xattn_g3, L0_xattn_be3, L1_xattn_ln1_g, L1_xattn_ln1_b, L1_xattn_ln2_g, L1_xattn_ln2_b, L1_xattn_ln3_g, L1_xattn_ln3_b, L1_xattn_q1_w, L1_xattn_k1_w, L1_xattn_v1_w, L1_xattn_o1_w, L1_xattn_o1_b, L1_xattn_q2_w, L1_xattn_k2_w, L1_xattn_v2_w, L1_xattn_o2_w, L1_xattn_o2_b, L1_xattn_ff1_w, L1_xattn_ff1_b, L1_xattn_ff2_w, L1_xattn_ff2_b):
    import jax
    import jax.numpy as jnp

    def _L0_xattn_ref(x, context, Wq1, Wk1, Wv1, Wo1, bo1, Wq2, Wk2, Wv2, Wo2, bo2, Wp, bp, W2, b2, g1, be1, g2, be2, g3, be3):
        import jax, jax.numpy as jnp
        import numpy as np
        DIM, HEADS, DHEAD, CTX_DIM = (128, 16, 64, 96)
        INNER = HEADS * DHEAD
        FF_HID = 4 * DIM
        EPS = 1e-05

        def _ln(x, g, b):
            mu = jnp.mean(x, axis=-1, keepdims=True)
            var = jnp.mean(jnp.square(x - mu), axis=-1, keepdims=True)
            return (x - mu) * jax.lax.rsqrt(var + EPS) * g + b

        def _attn(x, ctx, Wq, Wk, Wv, Wo, bo):
            b, n, _ = x.shape
            m = ctx.shape[1]
            q = (x @ Wq).reshape(b, n, HEADS, DHEAD)
            k = (ctx @ Wk).reshape(b, m, HEADS, DHEAD)
            v = (ctx @ Wv).reshape(b, m, HEADS, DHEAD)
            scale = DHEAD ** (-0.5)
            sim = jnp.einsum('bihd,bjhd->bhij', q, k) * scale
            attn = jax.nn.softmax(sim, axis=-1)
            out = jnp.einsum('bhij,bjhd->bihd', attn, v).reshape(b, n, INNER)
            return out @ Wo + bo
        h = _ln(x, g1, be1)
        x = _attn(h, h, Wq1, Wk1, Wv1, Wo1, bo1) + x
        h = _ln(x, g2, be2)
        x = _attn(h, context, Wq2, Wk2, Wv2, Wo2, bo2) + x
        h = _ln(x, g3, be3)
        y = h @ Wp + bp
        a, gate = (y[..., :FF_HID], y[..., FF_HID:])
        x = a * jax.nn.gelu(gate, approximate=False) @ W2 + b2 + x
        return x

    def _L1_xattn_ref(x, context, ln1_g, ln1_b, ln2_g, ln2_b, ln3_g, ln3_b, q1_w, k1_w, v1_w, o1_w, o1_b, q2_w, k2_w, v2_w, o2_w, o2_b, ff1_w, ff1_b, ff2_w, ff2_b):
        import jax, jax.numpy as jnp
        import numpy as np
        B, N, D, H, M, CD = (2, 256, 128, 16, 77, 96)
        DH = D // H
        FF = 4 * D
        NBITS = 8
        EPS = 1e-05

        def fake_quant_w(w, n_bits=NBITS):
            levels = 2 ** n_bits - 1
            mn = jnp.min(w)
            mx = jnp.max(w)
            delta = (mx - mn) / levels
            zp = jnp.round(-mn / delta)
            wq = jnp.clip(jnp.round(w / delta) + zp, 0, levels)
            wdq = (wq - zp) * delta
            return w + jax.lax.stop_gradient(wdq - w)

        def layernorm(x, g, b):
            mu = jnp.mean(x, axis=-1, keepdims=True)
            var = jnp.mean((x - mu) ** 2, axis=-1, keepdims=True)
            return (x - mu) * jax.lax.rsqrt(var + EPS) * g + b

        def linear(x, w, b=None):
            y = x @ fake_quant_w(w).T
            return y if b is None else y + b

        def cross_attn(x, ctx, qw, kw, vw, ow, ob):
            Bq, Nq, _ = x.shape
            Nk = ctx.shape[1]
            q = linear(x, qw).reshape(Bq, Nq, H, DH)
            k = linear(ctx, kw).reshape(Bq, Nk, H, DH)
            v = linear(ctx, vw).reshape(Bq, Nk, H, DH)
            scale = DH ** (-0.5)
            sim = jnp.einsum('bihd,bjhd->bhij', q, k) * scale
            attn = jax.nn.softmax(sim, axis=-1)
            out = jnp.einsum('bhij,bjhd->bihd', attn, v).reshape(Bq, Nq, D)
            return linear(out, ow, ob)

        def geglu_ff(x, w1, b1, w2, b2):
            h = linear(x, w1, b1)
            hidden, gate = jnp.split(h, 2, axis=-1)
            return linear(hidden * jax.nn.gelu(gate), w2, b2)
        x = cross_attn(layernorm(x, ln1_g, ln1_b), layernorm(x, ln1_g, ln1_b), q1_w, k1_w, v1_w, o1_w, o1_b) + x
        x = cross_attn(layernorm(x, ln2_g, ln2_b), context, q2_w, k2_w, v2_w, o2_w, o2_b) + x
        x = geglu_ff(layernorm(x, ln3_g, ln3_b), ff1_w, ff1_b, ff2_w, ff2_b) + x
        return x
    x = _L0_xattn_ref(x, ctx_768, L0_xattn_Wq1, L0_xattn_Wk1, L0_xattn_Wv1, L0_xattn_Wo1, L0_xattn_bo1, L0_xattn_Wq2, L0_xattn_Wk2, L0_xattn_Wv2, L0_xattn_Wo2, L0_xattn_bo2, L0_xattn_Wp, L0_xattn_bp, L0_xattn_W2, L0_xattn_b2, L0_xattn_g1, L0_xattn_be1, L0_xattn_g2, L0_xattn_be2, L0_xattn_g3, L0_xattn_be3)
    x = _L1_xattn_ref(x, ctx_768, L1_xattn_ln1_g, L1_xattn_ln1_b, L1_xattn_ln2_g, L1_xattn_ln2_b, L1_xattn_ln3_g, L1_xattn_ln3_b, L1_xattn_q1_w, L1_xattn_k1_w, L1_xattn_v1_w, L1_xattn_o1_w, L1_xattn_o1_b, L1_xattn_q2_w, L1_xattn_k2_w, L1_xattn_v2_w, L1_xattn_o2_w, L1_xattn_o2_b, L1_xattn_ff1_w, L1_xattn_ff1_b, L1_xattn_ff2_w, L1_xattn_ff2_b)
    return x

_drawn_inputs = setup_inputs


def setup_inputs(seed=0):
    import zlib

    import numpy as np

    out = dict(_drawn_inputs(seed))
    spreads = {'L0_xattn_bo1': (0.0, 0.1),
     'L0_xattn_bo2': (0.0, 0.1),
     'L0_xattn_bp': (0.0, 0.1),
     'L0_xattn_b2': (0.0, 0.1),
     'L0_xattn_g1': (1.0, 0.2),
     'L0_xattn_be1': (0.0, 0.1),
     'L0_xattn_g2': (1.0, 0.2),
     'L0_xattn_be2': (0.0, 0.359),
     'L0_xattn_g3': (1.0, 0.2),
     'L0_xattn_be3': (0.0, 0.1),
     'L1_xattn_o1_b': (0.0, 0.267),
     'L1_xattn_o2_b': (0.0, 0.1),
     'L1_xattn_ff1_b': (0.0, 0.8),
     'L1_xattn_ff2_b': (0.0, 0.8)}
    factors = {'L1_xattn_ln1_g': 8.0,
     'L1_xattn_ln1_b': 8.0,
     'L1_xattn_ln2_g': 8.0,
     'L1_xattn_ln2_b': 8.0,
     'L1_xattn_ln3_g': 8.0,
     'L1_xattn_ln3_b': 8.0,
     'L1_xattn_q1_w': 8.0,
     'L1_xattn_k1_w': 8.0,
     'L1_xattn_v1_w': 3.364,
     'L1_xattn_o1_w': 3.261,
     'L1_xattn_q2_w': 8.0,
     'L1_xattn_k2_w': 8.0,
     'L1_xattn_v2_w': 3.378,
     'L1_xattn_o2_w': 3.781,
     'L1_xattn_ff1_w': 5.246,
     'L1_xattn_ff2_w': 5.198}
    for name, (base, spread) in spreads.items():
        noise = np.random.default_rng([zlib.crc32(name.encode()), seed]).standard_normal(out[name].shape)
        drawn = base * np.exp(spread * noise) if base else spread * noise
        out[name] = jnp.asarray(drawn.astype(out[name].dtype))
    for name, factor in factors.items():
        out[name] = (out[name] * factor).astype(out[name].dtype)
    return out
```

```python
from contextlib import ExitStack

import numpy as np

import concourse.bass as bass
from concourse import mybir

F32 = mybir.dt.float32
F32R = mybir.dt.float32r
ALU = mybir.AluOpType
ACT = mybir.ActivationFunctionType
AX = mybir.AxisListType

NB, T, D, C, H = 4, 256, 128, 96, 16
DH0, DH1 = 64, 8
NCH = 4
EPS = 1e-5
LEVELS = 255.0
ROUND = 12582912.0
NS, NP, RING = 3, 6, 12
UNITS = 4 * NB
PAIRS = H // 2
L1W = ["q1", "k1", "v1", "o1", "q2", "o2", "k2", "v2"]
FULL = 6
SPLIT = {"q1": 0, "k1": 1, "q2": 2, "k2": 3}


def make_plan():
    plan = []

    def merge(main, side):
        n = max(len(main), 1)
        items = [(8.0 * i / n, 0, i, s) for i, s in enumerate(main)]
        items += [(pos, 1, i, s) for i, (pos, s) in enumerate(side)]
        plan.extend(s for *_, s in sorted(items, key=lambda x: x[:3]))

    def attention_inputs(u, side):
        if u >= UNITS:
            return
        if u < 8:
            for p in range(PAIRS):
                side.append((0.2 + 0.85 * p, ("q", u, p)))
                for ic in range(2):
                    side.append((1.2 + 0.85 * p + 0.25 * ic, ("smax", u, 2 * p + ic)))
            side.append((4.4, ("mT", u, 0)))
            side.append((7.8, ("mT", u, 1)))
            side.append((4.6, ("v", u, 0)))
            side.append((5.1, ("v", u, 1)))
        else:
            for p in range(PAIRS):
                for ic in range(2):
                    side.append((2.5 + 0.6 * p + 0.3 * ic, ("smax", u, 2 * p + ic)))
            side.append((5.3, ("mT", u, 0)))
            side.append((7.5, ("mT", u, 1)))
            side.append((1.0, ("v", u, 0)))

    plan += [("A", 0, 0), ("ln", 0, 0), ("A", 0, 1), ("xh", 0, 0), ("A", 0, 2), ("A", 0, 3),
             ("hT", 0, 0), ("wsplit", 0, 0)]
    for p in range(PAIRS):
        plan.append(("q", 0, p))
        if p:
            plan += [("smax", 0, 2 * p - 2), ("smax", 0, 2 * p - 1)]
        if p == 5:
            plan.append(("mT", 0, 0))
    plan += [("smax", 0, 14), ("smax", 0, 15), ("v", 0, 0), ("mT", 0, 1), ("v", 0, 1)]
    plan += [("st", 0, 0), ("st", 0, 1)]

    for u in range(UNITS + 2):
        main, side = [], []
        if u < UNITS:
            for p in range(PAIRS):
                for jc in range(2):
                    if p + 1 < PAIRS:
                        main.append(("st", u, 2 * p + 2 + jc))
                    elif u + 1 < UNITS:
                        main.append(("st", u + 1, jc))
                if u < 8:
                    main.append(("pv", u, p))
                    if p % 2:
                        main.append(("L", u, p))
                elif p % 2:
                    main.append(("pv", u, p))
        if u < 3:
            side += [(0.0, ("ln", 0, u + 1)), (0.05, ("xh", 0, u + 1)), (0.1, ("hT", 0, u + 1))]
        if u < 8:
            side += [(0.12, ("v", u, 2)), (0.6, ("v", u, 3))]
        if u == 0:
            side.append((1.0, ("load", 1, 0)))
        if u == 1:
            side += [(1.0 + 0.5 * k, ("A", 1, k)) for k in range(4)] + [(3.0, ("wsplit", 1, 0))]
        if u == 2:
            side.append((1.0, ("load", 2, 0)))
        if u == 4:
            side += [(1.0, ("wsplit", 2, 0)), (1.1, ("load", 3, 0)), (4.0, ("quant", 0, 0))]
        if u == 7:
            side.append((1.0, ("load", 4, 0)))
        if u == 9:
            side.append((1.0, ("quant", 1, 0)))
        if 7 <= u <= 10:
            side.append((0.7, ("qk", u + 1, 0)))
            side.append((1.0, ("stack", u + 1, 0)))
        if 10 <= u <= 13:
            side.append((5.0, ("qk", u + 2, 0)))
        if 11 <= u <= 14:
            side.append((0.05, ("stack", u + 1, 0)))
        attention_inputs(u + 1, side)
        c = u - 1
        if 0 <= c < 8:
            side += [(0.3, ("rcp", c, 0)), (1.3, ("rread", c, 0)), (3.6, ("wo", c, 0))]
            k = 1 + c // 4
            side += [(4.0, ("ln", k, c % 4)), (4.7, ("xh", k, c % 4)), (5.5, ("hT", k, c % 4))]
        elif 8 <= c < UNITS:
            side += [(0.8, ("uT", c, 0)), (1.2, ("uT", c, 1)), (1.8, ("oT", c, 0)), (2.4, ("wo", c, 0))]
            k = 2 + c // 4
            side += [(2.7, ("ln", k, c % 4)), (3.5, ("xh", k, c % 4)), (4.3, ("hT", k, c % 4))]
        for layer, first in ((0, 6), (1, 14)):
            b = u - first
            if 0 <= b < NB:
                f = 4 * layer + b
                side += [(0.4 + 0.45 * c4, ("ff1", f, c4)) for c4 in range(NCH)] + [(2.3, ("ff2", f, 0))]
                if layer == 0:
                    at = 2.5 if u < 9 else 3.7
                    side += [(at, ("ln", 3, b)), (at + 0.7, ("xh", 3, b)), (at + 1.4, ("hT", 3, b))]
                else:
                    side.append((3.1, ("out", b, 0)))
        merge(main, side)
    return plan


GENERAL = {"A", "q", "smax", "mT", "v", "wo", "hT", "ff1", "ff2", "qk", "uT", "oT"}


def build(nc, x_in, ctx_in, wqk_in, wv_in, wo_in, wp_in, w2_in, l1_in, ff1_in, ff2_in, cols_in, rows_in, out):
    plan = make_plan()
    order, uses, n_of = {}, {}, {}
    for s in plan:
        order[s] = n_of.get(s[0], 0)
        n_of[s[0]] = order[s] + 1
        if s[0] in GENERAL:
            uses[s] = len(uses)

    ctx = ExitStack()
    with ctx:
        def sb(name, shape, dt=F32, scope=ctx):
            return scope.enter_context(nc.sbuf_tensor(name, shape, dt))

        def sem(name):
            return ctx.enter_context(nc.semaphore(name))

        x = sb("x", [D, 2 * NB, D])
        hh = sb("h_hi", [D, NB, T], F32R)
        hl = sb("h_lo", [D, NB, T], F32R)
        hf = sb("h_full", [D, 2, T])
        chi = sb("ctx_hi", [C + 1, NB * T], F32R)
        clo = sb("ctx_lo", [C, NB * T], F32R)
        Qa = [sb(f"q_hi{i}", [D, H, T], F32R) for i in range(2)]
        Qb = [sb(f"q_lo{i}", [D, H, T], F32R) for i in range(2)]
        V = sb("v", [D, 2, H * DH0])
        Pr = [sb(f"p{i}", [D, 2 * T]) for i in range(NP)]
        U = sb("u", [D, RING, T])
        R = sb("r", [D, PAIRS, T])
        Rc = sb("r_rows", [D, T])
        Wo = [sb(f"wo{a}", [D, PAIRS, D]) for a in range(2)]
        stage = sb("stage", [D, 3, 1024])
        V1 = [w.rearrange("p (j h r) -> p j h r", j=2, h=H) for w in (stage[:, 2, :], V[:, 0, :])]
        Mt = [sb(f"m{i}", [D, 2, T], F32R) for i in range(2)]
        negm = [sb(f"negmax{i}", [D, 2, H]) for i in range(2)]
        W2 = [sb("w2_0", [D, NCH, D]), None]
        cols = sb("cols", [D, 12 + 16])
        rows = sb("rows", [D, 6, D])
        gl = sb("gelu", [D, T])
        xhat = sb("xhat", [D, 2, D])
        ident = sb("ident", [D, D])
        ident_r = sb("ident_r", [D, D], F32R)
        lsel = sb("l_select", [D, 4, 32])
        bst = sb("bn_stats", [D, 2, 6])
        mv = sb("bn_mv", [D, 2, 2])
        rs = sb("rstd", [D, 2])
        rs0 = sb("var_eps", [D, 2])
        mhalf = sb("mhalf", [D, 2])
        qs = sb("quant_scalars", [D, 8, 16])

        early = ExitStack()
        A = [[sb("a0_hi", [D, H, D], F32R, early), sb("a0_lo", [D, H, D], F32R, early)]]
        Wv = [[sb("wv0_hi", [D, 1024], F32R, early), sb("wv0_lo", [D, 1024], F32R, early)]]
        early.close()
        Wf = [[sb("wp_hi", [D, 1024], F32R), sb("wp_lo", [D, 1024], F32R)]]
        L1hi = sb("l1w_hi", [D, 4, D], F32R)
        L1lo = sb("l1w_lo", [D, 4, D], F32R)
        hf1 = sb("h_full_l1", [D, NB, T])
        gT = sb("g_t", [D, NCH, T])
        L1 = sb("l1w", [D, 8, D])
        early = ExitStack()
        A.append([sb("a1_hi", [D, H, C], F32R, early), sb("a1_lo", [D, H, C], F32R, early)])
        Wv.append([sb("wv1_hi", [D, 1024], F32R, early), sb("wv1_lo", [D, 1024], F32R, early)])
        early.close()
        F1 = stage[:, 0, :]
        Wf.append([sb("ff1_hi", [D, 1024], F32R), sb("ff1_lo", [D, 1024], F32R)])
        W2[1] = sb("w2_1", [D, NCH, D])
        cf = sb("ctx_full", [C, NB * T])
        QKh = sb("qk_hi", [D, 2 * T], F32R)
        QKl = sb("qk_lo", [D, 2 * T], F32R)
        on = sb("o_norm", [D, 2, D])
        oT = sb("o_t", [D, T])
        r_dram = [nc.dram_tensor(f"r_scratch{i}", [H, T], F32).ap() for i in range(2)]
        qk_dram = [nc.dram_tensor(f"qk_scratch{i}", [2, D, 2 * T], F32).ap() for i in range(2)]
        ps = [ctx.enter_context(nc.psum_tensor(f"bank{i}", [D, 512], F32)) for i in range(8)]
        SB, UB, LB, GB = ps[0:3], ps[3:5], ps[5], ps[6:8]

        g_ready = [sem(f"g_ready{i}") for i in range(2)]
        g_free = [sem(f"g_free{i}") for i in range(2)]
        hi_done = sem("hi_done")
        st_done = sem("st_done")
        exp_done = sem("exp_done")
        p_used = sem("p_used")
        u_ready, u_free = sem("u_ready"), sem("u_free")
        r_done = sem("r_done")
        r_put = sem("r_put")
        r_got = sem("r_got")
        norm_done = sem("norm_done")
        ln_stats, ln_rstd = sem("ln_stats"), sem("ln_rstd")
        ln_applied, xb_done = sem("ln_applied"), sem("xb_done")
        h_split = sem("h_split")
        m_row = [[sem(f"m_row{i}{j}") for j in range(2)] for i in range(2)]
        consts = sem("consts")
        loaded = [sem(f"loaded{i}") for i in range(5)]
        x_in_sem = sem("x_in")
        misc_in = sem("misc_in")
        c_in = sem("c_in")
        c_split = sem("c_split")
        w_hi, w_lo = sem("w_hi"), sem("w_lo")
        qk_put = sem("qk_put")
        stacked = [sem(f"stacked{i}") for i in range(2)]
        zeroed = sem("zeroed")
        q_stats, q_all, q_scal, q_quant, q_split = (sem(n) for n in ("q_stats", "q_all", "q_scal", "q_quant", "q_split"))
        dve = sem("dve_chain")
        pool = sem("pool_chain")
        out_done = sem("out_done")

        def filled(eng, s):
            n = uses[s]
            eng.wait_ge(g_ready[n % 2], n // 2 + 1)

        def emptied(eng, s):
            n = uses[s]
            eng.wait_ge(g_free[n % 2], n // 2 + 1)

        def st_through(eng, u):
            eng.wait_ge(st_done, 16 * (u + 1))

        hi_count = {s: 0 for s in plan}
        run = 0
        for s in plan:
            if s[0] in ("A", "q", "hT", "ff1", "qk"):
                run += 1
            hi_count[s] = run

        def u_index(u, p):
            return 8 * u + p if u < 8 else 64 + 4 * (u - 8) + p // 2

        def u_end(u):
            return 8 * (u + 1) if u < 8 else 64 + 4 * (u - 7)

        def unit_of(idx):
            return idx // 8 if idx < 64 else 8 + (idx - 64) // 4

        def released(eng, n):
            if n < 128:
                eng.wait_ge(p_used, n // 4 + 1)
            else:
                eng.wait_ge(u_ready, 64 + (n - 128) // 4 + 1)

        def kdim(a):
            return D if a % 2 == 0 else C

        def a_heads(k):
            first = 8 * (k // 2) + k % 2
            return slice(first, first + 7, 2)

        def view3(ap, n):
            return ap.rearrange("p (a b) -> p a b", a=n)

        block = ctx.enter_context(nc.Block())

        @block.sync
        def _(sp):
            def load_attn(a):
                dk = kdim(a)
                sp.dma_start(view3(stage[:, 0, :], PAIRS), wqk_in[a][0]).then_inc(loaded[a], 16)
                sp.dma_start(view3(stage[:, 1, 0:PAIRS * dk], PAIRS), wqk_in[a][1]).then_inc(loaded[a], 16)
                sp.dma_start(stage[0:dk, 2, :], wv_in[a]).then_inc(loaded[a], 16)
                sp.dma_start(Wo[a][:, :, :], wo_in[a]).then_inc(loaded[a], 16)

            sp.dma_start(x[:, 0:2, :], x_in[:, 0:2, :]).then_inc(x_in_sem, 16)
            load_attn(0)
            sp.dma_start(cols[:, :], cols_in).then_inc(misc_in, 16)
            sp.dma_start(rows[:, :, :], rows_in.partition_broadcast(D)).then_inc(misc_in, 16)
            sp.dma_start(x[:, 2:8, :], x_in[:, 2:8, :]).then_inc(misc_in, 16)
            sp.dma_start(R[0:C, 0:4, :].rearrange("p a b -> p (a b)"), ctx_in).then_inc(c_in, 16)
            for s in plan:
                name, u, i = s
                if name == "load":
                    if u == 1:
                        emptied(sp, ("A", 0, 3))
                        sp.wait_ge(w_lo, 1)
                        load_attn(1)
                    elif u == 2:
                        sp.wait_ge(w_lo, 2)
                        emptied(sp, ("A", 1, 3))
                        sp.dma_start(stage[:, 0, :], wp_in).then_inc(loaded[2], 16)
                        sp.dma_start(W2[0][:, :, :], w2_in).then_inc(loaded[2], 16)
                    elif u == 3:
                        filled(sp, ("q", 3, 7))
                        filled(sp, ("v", 3, 3))
                        sp.dma_start(L1[:, 0:FULL, :], l1_in[0]).then_inc(loaded[3], 16)
                        sp.dma_start(L1[0:C, FULL:8, :], l1_in[1]).then_inc(loaded[3], 16)
                    elif u == 4:
                        filled(sp, ("q", 7, 7))
                        filled(sp, ("v", 7, 3))
                        sp.wait_ge(w_lo, 3)
                        sp.dma_start(F1, ff1_in).then_inc(loaded[4], 16)
                        sp.dma_start(W2[1][:, :, :], ff2_in).then_inc(loaded[4], 16)
                        sp.dma_start(cf[:, :], ctx_in).then_inc(loaded[4], 16)
                elif name == "rcp":
                    sp.wait_ge(r_done, u + 1)
                    if u >= 2:
                        sp.wait_ge(r_got, 32 * (u - 1))
                    by_head = r_dram[u % 2].rearrange("(k c) i -> c k i", c=4)
                    for c in range(4):
                        sp.dma_start(by_head[c], Rc[32 * c:32 * c + 4, :]).then_inc(r_put, 16)
                elif name == "rread":
                    sp.wait_ge(r_put, 64 * (u + 1))
                    if u >= 1:
                        sp.wait_ge(norm_done, 2 * u)
                    else:
                        sp.wait_ge(c_split, 2)
                    by_side = r_dram[u % 2].rearrange("(p a) i -> a p i", a=2)
                    for a in range(2):
                        sp.dma_start(R[64 * a:64 * a + 64, :, :],
                                     by_side[a].partition_broadcast(64)).then_inc(r_got, 16)
                elif name == "mT" and u >= 4:
                    emptied(sp, s)
                    st_through(sp, u - 2)
                    sp.dma_start(Qa[u % 2][C:C + 1, 8 * i:8 * i + 8, :].bitcast(F32), Mt[u % 2][0:8, i, :].bitcast(F32))\
                      .then_inc(m_row[u % 2][i], 16)
                elif name == "qk":
                    emptied(sp, s)
                    if order[s] >= 2:
                        sp.wait_ge(stacked[u % 2], 128 * (order[s] // 2))
                    sp.dma_start(qk_dram[u % 2][0], QKh[:, :].bitcast(F32)).then_inc(qk_put, 16)
                    sp.dma_start(qk_dram[u % 2][1], QKl[:, :].bitcast(F32)).then_inc(qk_put, 16)
                elif name == "stack":
                    sp.wait_ge(qk_put, 32 * (order[("qk", u, 0)] + 1))
                    st_through(sp, u - 2)
                    sc = qk_dram[u % 2].rearrange("s (h d) i -> s d h i", d=DH1)
                    for t in range(4):
                        sp.dma_start(Qa[u % 2][8 * t:8 * t + 8, :, :].bitcast(F32), sc[t // 2][:, :, 0:T])\
                          .then_inc(stacked[u % 2], 16)
                        sp.dma_start(Qb[u % 2][8 * t:8 * t + 8, :, :].bitcast(F32), sc[t % 2][:, :, T:2 * T])\
                          .then_inc(stacked[u % 2], 16)
                elif name == "out":
                    emptied(sp, ("ff2", 4 + u, 0))
                    sp.dma_start(out[:, 2 * u:2 * u + 2, :], x[:, 2 * u:2 * u + 2, :]).then_inc(out_done, 16)
            sp.wait_ge(out_done, 16 * NB)

        @block.gpsimd
        def _(g):
            chain, zeroes = [0], [0]

            def link(ins):
                ins.then_inc(pool, 1)
                chain[0] += 1
                g.wait_ge(pool, chain[0])

            link(g.memset(ident[:, :], 0.0))
            link(g.affine_select(out=ident[:, :], in_=ident[:, :], compare_op=ALU.not_equal, fill=1.0,
                                 base=0, pattern=[[-1, D]], channel_multiplier=1))
            link(g.memset(mhalf[:, :], -0.5))
            link(g.memset(lsel[:, :, :], 1.0))
            link(g.memset(lsel[:, :, 0:4], 0.0))
            for k in range(4):
                link(g.memset(lsel[:, k, k:k + 1], 1.0))
            link(g.memset(qs[:, :, :], -3.0e38))
            link(g.memset(chi[C:C + 1, :].bitcast(F32), 1.0))
            link(g.memset(Mt[0][:, :, :].bitcast(F32), 0.0))
            link(g.memset(Mt[1][:, :, :].bitcast(F32), 0.0))
            g.memset(rs0[:, :], 0.0).then_inc(consts, 1)
            g.wait_ge(consts, 1)

            def quantize(w, j, np_):
                sc = lambda r: qs[0:np_, r, j:j + 1]
                n = w.shape[1]
                t = stage[0:np_, 1, 0:n]
                link(g.tensor_scalar(t, w, sc(3), ROUND, ALU.mult, ALU.add))
                link(g.tensor_scalar(t, t, -ROUND, sc(4), ALU.add, ALU.add))
                link(g.tensor_scalar(t, t, 0.0, LEVELS, ALU.max, ALU.min))
                link(g.tensor_scalar(t, t, sc(4), sc(2), ALU.subtract, ALU.mult))
                link(g.tensor_tensor(t, t, w, ALU.subtract))
                link(g.tensor_tensor(w, w, t, ALU.add))

            for s in plan:
                name, u, i = s
                if name == "rread":
                    g.wait_ge(r_got, 32 * (u + 1))
                    g.wait_ge(u_free, u_end(u))
                    for half in range(2):
                        at = (8 * u + 4 * half) % RING
                        g.tensor_tensor(U[:, at:at + 4, :], U[:, at:at + 4, :],
                                        R[:, 4 * half:4 * half + 4, :], ALU.mult).then_inc(norm_done, 1)
                        g.wait_ge(norm_done, 2 * u + half + 1)
                elif name == "ln":
                    n = order[s]
                    g.wait_ge(ln_stats, n + 1)
                    link(g.tensor_scalar(rs0[:, :], mv[:, :, 1], EPS, None, ALU.add))
                    g.tensor_tensor(rs[:, :], rs0[:, :], mhalf[:, :], ALU.pow).then_inc(ln_rstd, 1)
                    g.wait_ge(ln_rstd, n + 1)
                elif name == "xh":
                    g.wait_ge(ln_applied, order[s] + 1)
                    if order[s] == 0:
                        g.wait_ge(misc_in, 48)
                    for t in range(2):
                        ins = g.tensor_tensor(x[:, 2 * i + t, :], x[:, 2 * i + t, :], rows[:, u, :], ALU.add)
                        if t == 0:
                            link(ins)
                    ins.then_inc(xb_done, 1)
                    g.wait_ge(xb_done, order[s] + 1)
                elif name == "quant":
                    g.wait_ge(q_stats, u + 1)
                    g.partition_all_reduce(qs[:, 1, :], qs[:, 0, :], D, bass.bass_isa.ReduceOp.max).then_inc(q_all, 1)
                    g.wait_ge(q_scal, u + 1)
                    if u == 0:
                        for j in range(8):
                            r = D if j < FULL else C
                            quantize(L1[0:r, j, :], j, r)
                    else:
                        quantize(F1, 0, D)
                        quantize(W2[1][:, :, :].rearrange("p a b -> p (a b)"), 1, D)
                    g.memset(qs[:, 7, 0:1], 0.0).then_inc(q_quant, 1)
                    g.wait_ge(q_quant, u + 1)
                elif name == "stack" and u in (8, 9):
                    st_through(g, u - 2)
                    for r in (32, 64):
                        link(g.memset(Qa[u % 2][r:r + 32, :, :].bitcast(F32), 0.0))
                    g.memset(Qb[u % 2][C:C + 1, :, :].bitcast(F32), 1.0).then_inc(zeroed, 1)
                    zeroes[0] += 1
                    g.wait_ge(zeroed, zeroes[0])
                elif name == "v" and u in (8, 9):
                    if u == 8:
                        g.wait_ge(w_lo, 2)
                    else:
                        g.wait_ge(u_ready, u_end(7))
                    w = V1[u % 2]
                    link(g.memset(w[:, :, :, DH1:32], 0.0))
                    g.memset(w[:, :, :, DH1:DH1 + 1], 1.0).then_inc(zeroed, 1)
                    zeroes[0] += 1
                    g.wait_ge(zeroed, zeroes[0])

        @block.scalar
        def _(act):
            act.wait_ge(c_in, 16)
            act.activation(chi[0:C, :], R[0:C, 0:4, :].rearrange("p a b -> p (a b)"), ACT.Copy).then_inc(c_split, 1)
            for s in plan:
                name, u, i = s
                if name in GENERAL:
                    bank = GB[uses[s] % 2]
                    free = g_free[uses[s] % 2]
                if name == "A":
                    filled(act, s)
                    dk = kdim(u)
                    act.activation(A[u][0][:, a_heads(i), 0:dk], view3(bank[:, :], 4)[:, :, 0:dk], ACT.Copy)\
                       .then_inc(hi_done, 1)
                elif name == "wsplit":
                    act.wait_ge(loaded[u], 64 if u < 2 else 32)
                    dst, src = (Wv[u][0], stage[0:kdim(u), 2, :]) if u < 2 else (Wf[0][0], stage[:, 0, :])
                    if u == 2:
                        filled(act, ("q", 3, 7))
                        filled(act, ("v", 3, 3))
                    act.activation(dst[0:src.shape[0], :], src, ACT.Copy).then_inc(w_hi, 1)
                elif name == "q":
                    filled(act, s)
                    if u >= 2:
                        st_through(act, u - 2)
                    dk = kdim(u // 4)
                    act.activation(Qa[u % 2][0:dk, 2 * i:2 * i + 2, :], view3(bank[0:dk, :], 2), ACT.Copy)\
                       .then_inc(hi_done, 1)
                elif name == "mT":
                    filled(act, s)
                    if u >= 2:
                        st_through(act, u - 2)
                        if u >= 6:
                            act.wait_ge(m_row[u % 2][i], 16 * ((u - 6) // 2 + 1))
                    act.activation(Mt[u % 2][0:8, i, :], bank[0:8, 0:T], ACT.Copy).then_inc(free, 1)
                elif name == "v":
                    if u >= 8:
                        filled(act, s)
                        if u >= 9:
                            act.wait_ge(u_ready, u_end(u - 2))
                        for jc in range(2):
                            ins = act.activation(V1[u % 2][:, jc, :, 0:DH1],
                                                 bank[:, jc * D:jc * D + D].rearrange("p (h d) -> p h d", d=DH1), ACT.Copy)
                        ins.then_inc(free, 1)
                    elif i % 2 == 0:
                        filled(act, s)
                        if u >= 1:
                            act.wait_ge(u_ready, u_index(u - 1, 4 * (i // 2) + 3) + 1)
                        act.activation(V[:, i % 2, 512 * (i // 2):512 * (i // 2) + 512], bank[:, :], ACT.Copy)\
                           .then_inc(free, 1)
                elif name == "st":
                    n = order[s]
                    act.wait_ge(st_done, n + 1)
                    if n >= NP:
                        released(act, n - NP)
                    act.activation(Pr[n % NP][:, :], SB[n % NS][:, :], ACT.Exp,
                                   scale=float(DH0 if u < 8 else DH1) ** -0.5).then_inc(exp_done, 1)
                elif name == "pv":
                    n = u_index(u, i)
                    act.wait_ge(u_ready, n + 1)
                    if n >= RING:
                        w = unit_of(n - RING)
                        filled(act, ("wo", w, 0) if w < 8 else ("uT", w, 1))
                    act.activation(U[:, n % RING, :], UB[n % 2][:, 0:T], ACT.Copy).then_inc(u_free, 1)
                elif name == "hT":
                    filled(act, s)
                    if order[s] == 0:
                        act.wait_ge(misc_in, 48)
                    act.activation(hh[:, i, :], bank[:, 0:T], ACT.Identity, bias=cols[:, 2 * u + 1:2 * u + 2],
                                   scale=cols[:, 2 * u:2 * u + 1]).then_inc(hi_done, 1)
                elif name == "ff1":
                    filled(act, s)
                    layer = u // 4
                    if order[s] >= 1:
                        prev = [q for q in plan if q[0] == "ff1"][order[s] - 1]
                        emptied(act, prev)
                    bias = cols[:, 12 + 8 * layer + 4 + i:12 + 8 * layer + 5 + i]
                    act.activation(gl[:, :], bank[:, 0:T], ACT.Gelu if layer == 0 else ACT.Gelu_apprx_tanh,
                                   bias=bias).then_inc(hi_done, 1)
                elif name == "qk":
                    filled(act, s)
                    if order[s] >= 1:
                        act.wait_ge(qk_put, 32 * order[s])
                    act.activation(QKh[:, :], bank[:, :], ACT.Copy).then_inc(hi_done, 1)
                elif name == "oT":
                    filled(act, s)
                    if u > 8:
                        filled(act, ("wo", u - 1, 0))
                    act.activation(oT[:, :], bank[:, 0:T], ACT.Copy).then_inc(free, 1)

        @block.vector
        def _(v):
            chain = [0]

            def link(ins):
                ins.then_inc(dve, 1)
                chain[0] += 1
                v.wait_ge(dve, chain[0])

            v.wait_ge(pool, 2)
            v.tensor_copy(ident_r[:, :], ident[:, :]).then_inc(consts, 1)
            v.wait_ge(c_split, 1)
            v.tensor_tensor(clo[:, :], R[0:C, 0:4, :].rearrange("p a b -> p (a b)"),
                            chi[0:C, :].bitcast(F32), ALU.subtract).then_inc(c_split, 1)
            for s in plan:
                name, u, i = s
                if name in GENERAL:
                    bank = GB[uses[s] % 2]
                    free = g_free[uses[s] % 2]
                if name == "A":
                    v.wait_ge(hi_done, hi_count[s])
                    dk = kdim(u)
                    dst = a_heads(i)
                    v.tensor_tensor(A[u][1][:, dst, 0:dk], view3(bank[:, :], 4)[:, :, 0:dk],
                                    A[u][0][:, dst, 0:dk].bitcast(F32), ALU.subtract).then_inc(free, 1)
                elif name == "wsplit":
                    v.wait_ge(w_hi, u + 1)
                    dst, src = (Wv[u], stage[0:kdim(u), 2, :]) if u < 2 else (Wf[0], stage[:, 0, :])
                    r = src.shape[0]
                    v.tensor_tensor(dst[1][0:r, :], src, dst[0][0:r, :].bitcast(F32), ALU.subtract).then_inc(w_lo, 1)
                elif name == "q":
                    v.wait_ge(hi_done, hi_count[s])
                    if u >= 2:
                        st_through(v, u - 2)
                    dk = kdim(u // 4)
                    dst = slice(2 * i, 2 * i + 2)
                    v.tensor_tensor(Qb[u % 2][0:dk, dst, :], view3(bank[0:dk, :], 2),
                                    Qa[u % 2][0:dk, dst, :].bitcast(F32), ALU.subtract).then_inc(free, 1)
                elif name == "smax":
                    filled(v, s)
                    p, ic = i // 2, i % 2
                    if u >= 2:
                        filled(v, ("mT", u - 2, p // 4))
                    v.tensor_reduce(negm[u % 2][:, ic, 2 * p:2 * p + 2], view3(bank[:, :], 2), AX.X, ALU.max,
                                    negate=True).then_inc(free, 1)
                elif name == "v":
                    if u < 8 and i % 2 == 1:
                        filled(v, s)
                        if u >= 1:
                            v.wait_ge(u_ready, u_index(u - 1, 4 * (i // 2) + 3) + 1)
                        v.tensor_copy(V[:, i % 2, 512 * (i // 2):512 * (i // 2) + 512], bank[:, :]).then_inc(free, 1)
                elif name == "rcp":
                    v.wait_ge(p_used, 4 * (u + 1))
                    if u >= 1:
                        v.wait_ge(r_put, 64 * u)
                    v.reciprocal(Rc[:, :], LB[:, 0:T]).then_inc(r_done, 1)
                elif name == "wo":
                    filled(v, s)
                    b = u % 4
                    v.wait_ge(xb_done, order[("xh", [0, 1, 3, 4][u // 4], b)] + 1)
                    v.tensor_tensor(x[:, 2 * b:2 * b + 2, :], view3(bank[:, 0:T], 2), x[:, 2 * b:2 * b + 2, :],
                                    ALU.add).then_inc(free, 1)
                elif name == "ff2":
                    filled(v, s)
                    b = u % 4
                    v.wait_ge(xb_done, order[("xh", 2 + 3 * (u // 4), b)] + 1)
                    v.tensor_tensor(x[:, 2 * b:2 * b + 2, :], view3(bank[:, 0:T], 2), x[:, 2 * b:2 * b + 2, :],
                                    ALU.add).then_inc(free, 1)
                elif name == "ln":
                    if u == 0:
                        v.wait_ge(x_in_sem, 16) if i == 0 else v.wait_ge(misc_in, 48)
                    elif u == 3:
                        emptied(v, ("ff2", i, 0))
                    else:
                        emptied(v, ("wo", {1: 0, 2: 4, 4: 8, 5: 12}[u] + i, 0))
                    n = order[s]
                    if n:
                        v.wait_ge(ln_applied, n)
                    for t in range(2):
                        ins = v.bn_stats(bst[:, t, :], x[:, 2 * i + t, :])
                        if t == 1:
                            link(ins)
                    v.bn_aggr(mv[:, 0, :], bst[:, 0, :])
                    v.bn_aggr(mv[:, 1, :], bst[:, 1, :]).then_inc(ln_stats, 1)
                elif name == "xh":
                    n = order[s]
                    v.wait_ge(ln_stats, n + 1)
                    v.wait_ge(ln_rstd, n + 1)
                    if n:
                        prev = [q for q in plan if q[0] == "hT"][n - 1]
                        filled(v, prev)
                    for t in range(2):
                        ins = v.tensor_scalar(xhat[:, t, :], x[:, 2 * i + t, :], mv[:, t, 0:1], rs[:, t:t + 1],
                                              ALU.subtract, ALU.mult)
                    ins.then_inc(ln_applied, 1)
                elif name == "hT":
                    v.wait_ge(hi_done, hi_count[s])
                    n = order[s]
                    dst = hf1[:, i, :] if u == 3 else hf[:, n % 2, :]
                    if n:
                        v.wait_ge(h_split, n)
                    v.tensor_scalar(dst, bank[:, 0:T], cols[:, 2 * u:2 * u + 1], cols[:, 2 * u + 1:2 * u + 2],
                                    ALU.mult, ALU.add).then_inc(free, 1)
                    emptied(v, s)
                    v.tensor_tensor(hl[:, i, :], dst, hh[:, i, :].bitcast(F32), ALU.subtract).then_inc(h_split, 1)
                elif name == "ff1":
                    v.wait_ge(hi_done, hi_count[s])
                    layer = u // 4
                    if u >= 1:
                        filled(v, ("ff2", u - 1, 0))
                    v.scalar_tensor_tensor(gT[:, i, :], bank[:, T:2 * T], cols[:, 12 + 8 * layer + i:13 + 8 * layer + i],
                                           gl[:, :], ALU.add, ALU.mult).then_inc(free, 1)
                elif name == "qk":
                    v.wait_ge(hi_done, hi_count[s])
                    if order[s] >= 1:
                        v.wait_ge(qk_put, 32 * order[s])
                    v.tensor_tensor(QKl[:, :], bank[:, :], QKh[:, :].bitcast(F32), ALU.subtract).then_inc(free, 1)
                elif name == "uT":
                    filled(v, s)
                    w = bank[:, :].rearrange("p (h r) -> p h r", r=32)
                    if u > 8:
                        filled(v, ("oT", u - 1, 0))
                    rec = qs[:, 5 + i, :]
                    link(v.reciprocal(rec, w[:, :, DH1]))
                    v.tensor_tensor(on[:, i, :].rearrange("p (h d) -> p h d", d=DH1), w[:, :, 0:DH1],
                                    rec.unsqueeze(2).to_broadcast([D, H, DH1]), ALU.mult).then_inc(free, 1)
                elif name == "quant":
                    v.wait_ge(loaded[3 + u], 32 if u == 0 else 48)
                    if u == 0:
                        parts = [(slice(0, FULL), L1[:, 0:FULL, :], D), (slice(FULL, 8), L1[0:C, FULL:8, :], C)]
                    else:
                        parts = [(slice(0, 1), F1, D), (slice(1, 2), W2[1][:, :, :], D)]
                    for sl, w, r in parts:
                        ax = AX.XY if (u == 1 and sl.start == 1) else AX.X
                        for o, op, neg in ((0, ALU.max, False), (8, ALU.min, True)):
                            link(v.tensor_reduce(qs[0:r, 0, sl.start + o:sl.stop + o], w, ax, op, negate=neg))
                    v.tensor_copy(qs[:, 7, 8:9], qs[:, 0, 0:1]).then_inc(q_stats, 1)
                    v.wait_ge(q_all, u + 1)
                    mx, mn = qs[:, 1, 0:8], qs[:, 1, 8:16]
                    if True:
                        link(v.tensor_tensor(qs[:, 2, 8:16], mx, mn, ALU.add))
                        link(v.tensor_scalar(qs[:, 2, 0:8], qs[:, 2, 8:16], 1.0 / LEVELS, None, ALU.mult))
                        link(v.reciprocal(qs[:, 3, 0:8], qs[:, 2, 0:8]))
                        link(v.tensor_tensor(qs[:, 4, 8:16], mn, qs[:, 3, 0:8], ALU.mult))
                        link(v.tensor_scalar(qs[:, 4, 0:8], qs[:, 4, 8:16], ROUND, None, ALU.add))
                        v.tensor_scalar(qs[:, 4, 0:8], qs[:, 4, 0:8], -ROUND, None, ALU.add).then_inc(q_scal, 1)
                    v.wait_ge(q_quant, u + 1)
                    if u == 0:
                        for nm, k in SPLIT.items():
                            j = L1W.index(nm)
                            r = D if j < FULL else C
                            link(v.tensor_copy(L1hi[0:r, k, :], L1[0:r, j, :]))
                            ins = v.tensor_tensor(L1lo[0:r, k, :], L1[0:r, j, :], L1hi[0:r, k, :].bitcast(F32), ALU.subtract)
                    else:
                        link(v.tensor_copy(Wf[1][0][:, :], F1))
                        ins = v.tensor_tensor(Wf[1][1][:, :], F1, Wf[1][0][:, :].bitcast(F32), ALU.subtract)
                    ins.then_inc(q_split, 1)

        @block.tensor
        def _(pe):
            def claim(s):
                n = uses[s]
                if n >= 2:
                    pe.wait_ge(g_free[n % 2], n // 2)
                return GB[n % 2]

            def three(dst, w, m, k, start=True, stop=True):
                pe.matmul(dst, w[0], m[0], start=start, stop=False, skip_group_check=True)
                pe.matmul(dst, w[1], m[0], start=False, stop=False, skip_group_check=True)
                return pe.matmul(dst, w[0], m[1], start=False, stop=stop, skip_group_check=True)

            pe.wait_ge(consts, 2)
            for s in plan:
                name, u, i = s
                if name in GENERAL:
                    bank = claim(s)
                    ready = g_ready[uses[s] % 2]
                if name == "A":
                    pe.wait_ge(loaded[u], 64)
                    dk = kdim(u)
                    wq, wk = view3(stage[:, 0, :], PAIRS), view3(stage[:, 1, 0:PAIRS * dk], PAIRS)
                    for j in range(4):
                        h = 8 * (i // 2) + 2 * j + i % 2
                        r = 64 * (i % 2)
                        ins = pe.matmul(bank[:, j * D:j * D + dk], wq[r:r + 64, h // 2, :], wk[r:r + 64, h // 2, :],
                                        start=True, stop=True)
                    ins.then_inc(ready, 1)
                elif name == "q":
                    a, b, dk = u // 4, u % 4, kdim(u // 4)
                    emptied(pe, ("A", a, 2 * (i // 4)))
                    emptied(pe, ("A", a, 2 * (i // 4) + 1))
                    pe.wait_ge(h_split, order[("hT", a, b)] + 1)
                    for j in range(2):
                        h = 2 * i + j
                        ins = three(bank[0:dk, j * T:j * T + T], [A[a][k][:, h, 0:dk] for k in range(2)],
                                    [hh[:, b, :], hl[:, b, :]], D)
                    ins.then_inc(ready, 1)
                elif name == "smax":
                    p, ic, b = i // 2, i % 2, u % 4
                    if u < 8:
                        emptied(pe, ("q", u, p))
                        dk = kdim(u // 4)
                    else:
                        pe.wait_ge(stacked[u % 2], 128 * ((u - 8) // 2 + 1))
                        pe.wait_ge(zeroed, {8: 1, 9: 3}.get(u, 4))
                        dk = C
                    for j in range(2):
                        h = 2 * p + j
                        keys = hh[:, b, :] if u < 4 else chi[0:C, b * T:b * T + T] if u < 8 else Qb[u % 2][0:C, h, :]
                        ins = pe.matmul(bank[:, j * T:j * T + T], Qa[u % 2][0:dk, h, ic * D:ic * D + D], keys,
                                        start=True, stop=True)
                    ins.then_inc(ready, 1)
                elif name == "mT":
                    emptied(pe, ("smax", u, 8 * i + 7))
                    for ic in range(2):
                        ins = pe.transpose(bank[0:8, ic * D:ic * D + D], negm[u % 2][:, ic, 8 * i:8 * i + 8], ident[:, :])
                    ins.then_inc(ready, 1)
                elif name == "v":
                    b = u % 4
                    if u < 8:
                        a, dk, half, jc = u // 4, kdim(u // 4), i // 2, i % 2
                        pe.wait_ge(w_lo, a + 1)
                        at = b * T + jc * D
                        if a == 0:
                            pe.wait_ge(h_split, order[("hT", 0, b)] + 1)
                            keys = [w[:, b, jc * D:jc * D + D] for w in (hh, hl)]
                        else:
                            pe.wait_ge(c_split, 2)
                            keys = [chi[0:C, at:at + D], clo[:, at:at + D]]
                        w = [Wv[a][k][0:dk, 512 * half:512 * half + 512] for k in range(2)]
                        ins = three(bank[:, :], keys, w, dk)
                    else:
                        pe.wait_ge(q_quant, 1)
                        j = L1W.index("v1" if u < 12 else "v2")
                        if u < 12:
                            pe.wait_ge(h_split, order[("hT", 3, b)] + 1)
                        else:
                            pe.wait_ge(loaded[4], 48)
                        for jc in range(2):
                            at = b * T + jc * D
                            keys = hf1[:, b, jc * D:jc * D + D] if u < 12 else cf[:, at:at + D]
                            ins = pe.matmul(bank[:, jc * D:jc * D + D], keys, L1[0:D if u < 12 else C, j, :],
                                            start=True, stop=True)
                    ins.then_inc(ready, 1)
                elif name == "st":
                    n, p, jc, b = order[s], i // 2, i % 2, u % 4
                    if n >= NS:
                        pe.wait_ge(exp_done, n - NS + 1)
                    emptied(pe, ("mT", u, p // 4))
                    if u >= 4:
                        pe.wait_ge(m_row[u % 2][p // 4], 16 * ((u - 4) // 2 + 1))
                    bank = SB[n % NS]
                    at = b * T + jc * D
                    q2 = [Qa[u % 2], Qb[u % 2]]
                    if u < 4:
                        emptied(pe, ("q", u, p))
                        three(bank[:, :], [hh[:, b, jc * D:jc * D + D], hl[:, b, jc * D:jc * D + D]],
                              [w[:, 2 * p:2 * p + 2, :] for w in q2], D, stop=False)
                        for j in range(2):
                            r = (2 * p + j) % 8
                            ins = pe.matmul(bank[:, j * T:j * T + T], ident_r[:, r:r + 1].to_broadcast([D, D]),
                                            Mt[u % 2][:, p // 4, :], start=False, stop=True, skip_group_check=True)
                    elif u < 8:
                        emptied(pe, ("q", u, p))
                        pe.wait_ge(c_split, 2)
                        q = [w[0:C, 2 * p:2 * p + 2, :] for w in q2]
                        pe.matmul(bank[:, :], chi[0:C + 1, at:at + D], Qa[u % 2][0:C + 1, 2 * p:2 * p + 2, :],
                                  start=True, stop=False, skip_group_check=True)
                        pe.matmul(bank[:, :], clo[:, at:at + D], q[0], start=False, stop=False, skip_group_check=True)
                        ins = pe.matmul(bank[:, :], chi[0:C, at:at + D], q[1], start=False, stop=True,
                                        skip_group_check=True)
                    else:
                        for j in range(2):
                            h = 2 * p + j
                            ins = pe.matmul(bank[:, j * T:j * T + T], Qb[u % 2][0:C + 1, h, jc * D:jc * D + D],
                                            Qa[u % 2][0:C + 1, h, :], start=True, stop=True)
                    ins.then_inc(st_done, 1)
                elif name == "pv":
                    n = u_index(u, i)
                    bank = UB[n % 2]
                    if n >= 2:
                        pe.wait_ge(u_free, n - 1)
                    pe.wait_ge(exp_done, order[("st", u, 2 * i + 1)] + 1)
                    if u < 8:
                        emptied(pe, ("v", u, 2 * (i // 4)))
                        emptied(pe, ("v", u, 2 * (i // 4) + 1))
                        for jc in range(2):
                            pr = Pr[order[("st", u, 2 * i + jc)] % NP]
                            for j in range(2):
                                h = 2 * i + j
                                ins = pe.matmul(bank[64 * j:64 * j + 64, 0:T], V[:, jc, DH0 * h:DH0 * h + DH0],
                                                pr[:, j * T:j * T + T], start=(jc == 0), stop=(jc == 1))
                    else:
                        emptied(pe, ("v", u, 0))
                        pe.wait_ge(zeroed, {8: 2, 9: 4}.get(u, 4))
                        for jc in range(2):
                            for c in range(4):
                                h = 4 * (i // 2) + c
                                pr = Pr[order[("st", u, 2 * (h // 2) + jc)] % NP]
                                ins = pe.matmul(bank[32 * c:32 * c + 32, 0:T], V1[u % 2][:, jc, h, :],
                                                pr[:, (h % 2) * T:(h % 2) * T + T], start=(jc == 0), stop=(jc == 1),
                                                tile_position=(0, 32 * c))
                    ins.then_inc(u_ready, 1)
                elif name == "L":
                    k = i // 2
                    if k == 0 and u >= 1:
                        pe.wait_ge(r_done, u)
                    for jc in range(2):
                        for c in range(4):
                            h = 4 * k + c
                            pr = Pr[order[("st", u, 2 * (h // 2) + jc)] % NP]
                            ins = pe.matmul(LB[32 * c:32 * c + 32, 0:T], lsel[:, k, :], pr[:, (h % 2) * T:(h % 2) * T + T],
                                            start=(k == 0 and jc == 0), stop=(k == 3 and jc == 1),
                                            tile_position=(0, 32 * c))
                    ins.then_inc(p_used, 1)
                elif name == "wo":
                    if u < 8:
                        pe.wait_ge(norm_done, 2 * (u + 1))
                        for t in range(2):
                            for p in range(PAIRS):
                                ins = pe.matmul(bank[:, t * D:t * D + D], U[:, (8 * u + p) % RING, t * D:t * D + D],
                                                Wo[u // 4][:, p, :], start=(p == 0), stop=(p == PAIRS - 1))
                    else:
                        emptied(pe, ("oT", u, 0))
                        j = L1W.index("o1" if u < 12 else "o2")
                        for t in range(2):
                            ins = pe.matmul(bank[:, t * D:t * D + D], oT[:, t * D:t * D + D], L1[:, j, :],
                                            start=True, stop=True)
                    ins.then_inc(ready, 1)
                elif name == "hT":
                    pe.wait_ge(ln_applied, order[s] + 1)
                    for t in range(2):
                        ins = pe.transpose(bank[:, t * D:t * D + D], xhat[:, t, :], ident[:, :])
                    ins.then_inc(ready, 1)
                elif name == "ff1":
                    layer, b = u // 4, u % 4
                    pe.wait_ge(h_split, order[("hT", 2 + 3 * layer, b)] + 1)
                    if layer == 0:
                        pe.wait_ge(w_lo, 3)
                    else:
                        pe.wait_ge(q_split, 2)
                    for half, ch in ((0, NCH + i), (1, i)):
                        ins = three(bank[:, half * T:half * T + T], [w[:, ch * D:ch * D + D] for w in Wf[layer]],
                                    [hh[:, b, :], hl[:, b, :]], D)
                    ins.then_inc(ready, 1)
                elif name == "ff2":
                    layer = u // 4
                    emptied(pe, ("ff1", u, NCH - 1))
                    if layer == 0:
                        pe.wait_ge(loaded[2], 32)
                    else:
                        pe.wait_ge(q_quant, 2)
                    for t in range(2):
                        for c in range(NCH):
                            ins = pe.matmul(bank[:, t * D:t * D + D], gT[:, c, t * D:t * D + D], W2[layer][:, c, :],
                                            start=(c == 0), stop=(c == NCH - 1))
                    ins.then_inc(ready, 1)
                elif name == "qk":
                    b, cross = u % 4, u >= 12
                    pe.wait_ge(q_split, 1)
                    pe.wait_ge(h_split, order[("hT", 4 if cross else 3, b)] + 1)
                    for half, nm in ((0, "q2" if cross else "q1"), (1, "k2" if cross else "k1")):
                        r = C if nm == "k2" else D
                        k = SPLIT[nm]
                        src = [chi[0:C, b * T:b * T + T], clo[:, b * T:b * T + T]] if nm == "k2" else [hh[:, b, :], hl[:, b, :]]
                        ins = three(bank[:, half * T:half * T + T], [L1hi[0:r, k, :], L1lo[0:r, k, :]], src, r)
                    ins.then_inc(ready, 1)
                elif name == "uT":
                    pe.wait_ge(u_free, u_end(u))
                    for g4 in range(4):
                        at = (64 + 4 * (u - 8) + g4) % RING
                        ins = pe.transpose(bank[:, g4 * D:g4 * D + D], U[:, at, i * D:i * D + D], ident[:, :])
                    ins.then_inc(ready, 1)
                elif name == "oT":
                    emptied(pe, ("uT", u, 0))
                    emptied(pe, ("uT", u, 1))
                    for t in range(2):
                        ins = pe.transpose(bank[:, t * D:t * D + D], on[:, t, :], ident[:, :])
                    ins.then_inc(ready, 1)


def kernel(**inputs):
    import concourse.bacc as bacc
    from concourse.bass_utils import run_bass_kernel_spmd

    a = {k: np.asarray(v) for k, v in inputs.items()}
    L0, L1n = "L0_xattn_", "L1_xattn_"
    flat = lambda w: np.ascontiguousarray(w)
    by_p = lambda w, n: flat(w.reshape(n, D, -1).transpose(1, 0, 2))
    arrays = {
        "x_tok": by_p(a["x"], 2 * NB),
        "ctx_t": flat(a["ctx_768"].reshape(NB * T, C).T),
        "wq_t1": by_p(a[L0 + "Wq1"].T, PAIRS), "wk_t1": by_p(a[L0 + "Wk1"].T, PAIRS),
        "wq_t2": by_p(a[L0 + "Wq2"].T, PAIRS), "wk_t2": by_p(a[L0 + "Wk2"].T, PAIRS),
        "wv1": a[L0 + "Wv1"], "wv2": a[L0 + "Wv2"],
        "wo1": by_p(a[L0 + "Wo1"], PAIRS), "wo2": by_p(a[L0 + "Wo2"], PAIRS),
        "wp": a[L0 + "Wp"], "w2": by_p(a[L0 + "W2"], NCH),
        "l1_full": flat(np.stack([a[f"{L1n}{n}_w"].T for n in L1W[:FULL]], 1)),
        "l1_ctx": flat(np.stack([a[f"{L1n}{n}_w"].T for n in L1W[FULL:]], 1)),
        "ff1_t": flat(a[L1n + "ff1_w"].T), "ff2_t": by_p(a[L1n + "ff2_w"].T, NCH),
        "cols": flat(np.concatenate([np.stack([
            a[L0 + "g1"], a[L0 + "be1"], a[L0 + "g2"], a[L0 + "be2"], a[L0 + "g3"], a[L0 + "be3"],
            a[L1n + "ln1_g"], a[L1n + "ln1_b"], a[L1n + "ln2_g"], a[L1n + "ln2_b"], a[L1n + "ln3_g"], a[L1n + "ln3_b"],
        ], 1), a[L0 + "bp"].reshape(8, D).T, a[L1n + "ff1_b"].reshape(8, D).T], 1)),
        "rows": flat(np.stack([a[L0 + "bo1"], a[L0 + "bo2"], a[L0 + "b2"],
                               a[L1n + "o1_b"], a[L1n + "o2_b"], a[L1n + "ff2_b"]], 0)),
    }
    nc = bacc.Bacc("TRN2", target_bir_lowering=False, num_devices=1)
    t = {n: nc.dram_tensor("in_" + n, w.shape, F32, kind="ExternalInput").ap() for n, w in arrays.items()}
    out = nc.dram_tensor("out", (D, 2 * NB, D), F32, kind="ExternalOutput").ap()
    build(nc, t["x_tok"], t["ctx_t"], [(t["wq_t1"], t["wk_t1"]), (t["wq_t2"], t["wk_t2"])], [t["wv1"], t["wv2"]],
          [t["wo1"], t["wo2"]], t["wp"], t["w2"], (t["l1_full"], t["l1_ctx"]), t["ff1_t"], t["ff2_t"],
          t["cols"], t["rows"], out)
    r = run_bass_kernel_spmd(nc, [{"in_" + n: w for n, w in arrays.items()}], core_ids=[0])
    got = r.results[0]["out"]
    return flat(got.transpose(1, 0, 2)).reshape(NB, T, D)
```

```python
from contextlib import ExitStack

import numpy as np

import concourse.bass as bass
from concourse import mybir

F32 = mybir.dt.float32
F32R = mybir.dt.float32r
ALU = mybir.AluOpType
ACT = mybir.ActivationFunctionType
AX = mybir.AxisListType

NB, T, D, C, H = 4, 256, 128, 96, 16
DH0, DH1 = 64, 8
NCH = 4
EPS = 1e-5
LEVELS = 255.0
ROUND = 12582912.0
NS, NG, NP, RING = 3, 3, 6, 12
UNITS = 4 * NB
PAIRS = H // 2
L1W = ["q1", "k1", "v1", "o1", "q2", "o2", "k2", "v2"]
FULL = 6
SPLIT = {"q1": 0, "k1": 1, "q2": 2, "k2": 3}


def make_plan():
    plan = []

    def merge(main, side):
        n = max(len(main), 1)
        items = [(8.0 * i / n, 0, i, s) for i, s in enumerate(main)]
        items += [(pos, 1, i, s) for i, (pos, s) in enumerate(side)]
        plan.extend(s for *_, s in sorted(items, key=lambda x: x[:3]))

    def attention_inputs(u, side):
        if u >= UNITS:
            return
        if u < 8:
            for m in range(4):
                side += [(0.45 + 2 * m, ("k", u, m)), (0.95 + 2 * m, ("q", u, m))]
            side += [(2 * (i // 4) + (2.1, 2.7, 3.2, 3.5)[i % 4], ("smax", u, i)) for i in range(12)]
            side.append((5.95, ("mT", u, 0)))
            side += [(4.3, ("v", u, 0)), (6.3, ("v", u, 1))]
        elif u == 8:
            side += [(4.8 + 0.22 * i, ("smax", u, i)) for i in range(8)]
            side.append((6.7, ("mT", u, 0)))
            side.append((2.0, ("v", u, 0)))
        else:
            first, step = (1.8, 0.3) if u < 12 else (0.2, 0.43)
            side += [(first + step * i, ("smax", u, i)) for i in range(16)]
            side.append((first + step * 8.4, ("mT", u, 0)))
            side.append((first + step * 16.4, ("mT", u, 1)))
            side.append((1.0, ("v", u, 0)))

    def rest_of_inputs(u, side):
        if u <= 8:
            if u < 8:
                side += [((0.1, 0.7, 1.2, 1.5)[i % 4], ("smax", u, i)) for i in range(12, 16)]
            else:
                side += [(0.1 + 0.25 * (i - 8), ("smax", u, i)) for i in range(8, 16)]
            side.append((1.8 if u < 8 else 2.2, ("mT", u, 1)))
        if u < 8:
            side += [(0.4, ("v", u, 2)), (2.5, ("v", u, 3))]

    plan += [("ln", 0, 0), ("wsplit", 0, 0), ("xh", 0, 0), ("wsplit", 0, 1), ("hT", 0, 0),
             ("kpad", 0, 0), ("q", 0, 0), ("k", 0, 0), ("q", 0, 1), ("k", 0, 1), ("wsplit", 0, 2)]
    plan += [("smax", 0, i) for i in range(8)]
    plan += [("v", 0, 0), ("mT", 0, 0), ("v", 0, 1), ("q", 0, 2), ("k", 0, 2), ("smax", 0, 8), ("st", 0, 0), ("q", 0, 3), ("k", 0, 3),
             ("smax", 0, 9), ("st", 0, 1), ("smax", 0, 10), ("smax", 0, 11)]

    for u in range(UNITS + 2):
        main, side = [], []
        if u < UNITS:
            for p in range(PAIRS):
                for jc in range(2):
                    if p + 1 < PAIRS:
                        main.append(("st", u, 2 * p + 2 + jc))
                    elif u + 1 < UNITS:
                        main.append(("st", u + 1, jc))
                if u < 8:
                    main.append(("pv", u, p))
                    if p % 2:
                        main.append(("L", u, p))
                elif p % 2:
                    main.append(("pv", u, p))
        if u < 3:
            side += [(0.0, ("ln", 0, u + 1)), (0.05, ("xh", 0, u + 1)), (0.1, ("hT", 0, u + 1))]
        rest_of_inputs(u, side)
        if u == 0:
            side += [(0.9, ("csplit", 0, 0)), (1.0, ("load", 1, 0))]
        if u == 1:
            side += [(1.2 + 2.0 * k, ("wsplit", 1, k)) for k in range(3)]
        if u == 2:
            side.append((1.0, ("load", 2, 0)))
        if u == 3:
            side += [(2.7, ("wsplit", 2, 0)), (2.8, ("load", 3, 0)), (5.0, ("qstat", 0, 0)), (6.5, ("qscal", 0, 0))]
        if u in (4, 5):
            side += [((0.2, 2.4, 5.7, 7.0)[k], ("qw", 0, 4 * (u - 4) + k)) for k in range(4)]
        if u == 5:
            side.append((7.8, ("qsplit", 0, 0)))
        if u == 7:
            side.append((2.7, ("load", 4, 0)))
        if u == 9:
            side += [(1.0, ("qstat", 1, 0)), (3.0, ("qscal", 1, 0))]
        if u in (10, 11, 12):
            side += [((0.2, 1.4, 5.7, 7.0)[k], ("qw", 1, 4 * (u - 10) + k)) for k in range(4)]
        if u == 13:
            side.append((2.0, ("qsplit", 1, 0)))
        if 6 <= u <= 13:
            side.append((5.4 if u < 10 else 1.3, ("qk", u + 2, 0)))
        if u == 7:
            side += [(3.2, ("stack", 8, 0)), (7.1, ("stack", 8, 1)), (7.2, ("stack", 9, 2))]
        if 9 <= u <= 10:
            side.append((0.05, ("stack", u + 1, 2)))
        if 10 <= u <= 13:
            side.append((4.1, ("stack", u + 2, 0)))
        if 11 <= u <= 14:
            side.append((0.05, ("stack", u + 1, 1)))
        attention_inputs(u + 1, side)
        c = u - 1
        if 0 <= c < 8:
            side += [(0.3, ("rcp", c, 0)), (1.2, ("rread", c, 0)), (4.1, ("wo", c, 0))]
            k = 1 + c // 4
            side += [(4.5, ("ln", k, c % 4)), (4.9, ("xh", k, c % 4)), (5.3, ("hT", k, c % 4))]
        elif 8 <= c < UNITS:
            side += [(0.8, ("uT", c, 0)), (1.2, ("uT", c, 1)), (1.8, ("oT", c, 0)), (2.4, ("wo", c, 0))]
            k = 2 + c // 4
            side += [(2.7, ("ln", k, c % 4)), (3.5, ("xh", k, c % 4)), (4.3, ("hT", k, c % 4))]
        for layer, first in ((0, 6), (1, 14)):
            b = u - first
            if 0 <= b < NB:
                f = 4 * layer + b
                side += [(0.4 + 0.01 * c4, ("ff1", f, c4)) for c4 in range(NCH)] + [(1.6, ("ff2", f, 0))]
                if layer == 0:
                    at = 1.9 if u < 9 else 3.7
                    side += [(at, ("ln", 3, b)), (at + 0.7, ("xh", 3, b)), (at + 1.4, ("hT", 3, b))]
                else:
                    side.append((3.1, ("out", b, 0)))
        merge(main, side)
    return plan


GENERAL = {"q", "k", "smax", "mT", "v", "wo", "hT", "ff1", "ff2", "qk", "uT", "oT"}


def build(nc, x_in, ctx_in, w3_in, wo_in, wp_in, w2_in, l1_in, ff1_in, ff2_in, cols_in, rows_in, out):
    plan = make_plan()
    order, uses, n_of = {}, {}, {}
    in_bank, turn, last_denominators = [0] * (NG + 1), 0, 1
    for s in plan:
        order[s] = n_of.get(s[0], 0)
        n_of[s[0]] = order[s] + 1
        if s[0] in GENERAL:
            late = last_denominators < 0
            k = turn % (NG + late)
            turn = turn + 1
            uses[s] = (k, in_bank[k])
            in_bank[k] += 1
        elif s == ("rcp", 7, 0):
            last_denominators, turn = -1, NG

    ctx = ExitStack()
    with ctx:
        def sb(name, shape, dt=F32, scope=ctx):
            return scope.enter_context(nc.sbuf_tensor(name, shape, dt))

        def sem(name):
            return ctx.enter_context(nc.semaphore(name))

        x = sb("x", [D, 2 * NB, D])
        hh = sb("h_hi", [D, NB, T], F32R)
        hl = sb("h_lo", [D, NB, T], F32R)
        hf = sb("h_full", [D, 2, T])
        chi = sb("ctx_hi", [C, NB * T], F32R)
        clo = sb("ctx_lo", [C, NB * T], F32R)
        Q1, Q2, K1, K2 = (sb(n, [D, H, T], F32R) for n in ("q_hi_lo", "q_hi_max", "k_hi_hi", "k_lo_one"))
        QS, KS = [Q1, Q2], [K1, K2]
        V = sb("v", [D, 2, H * DH0])
        Pr = [sb(f"p{i}", [D, 2 * T]) for i in range(NP)]
        U = sb("u", [D, RING, T])
        R = sb("r", [D, PAIRS, T])
        Rc = sb("r_rows", [D, T])
        Wo = [sb(f"wo{a}", [D, PAIRS, D]) for a in range(2)]
        stage = sb("stage", [D, 3, 1024])
        V1 = [w.rearrange("p (j h r) -> p j h r", j=2, h=H) for w in (stage[:, 2, :], V[:, 0, :])]
        Mt = [sb(f"m{i}", [8, T], F32R) for i in range(2)]
        negm = [sb(f"negmax{i}", [D, 2, 2, 8]) for i in range(2)]
        W2 = [sb("w2_0", [D, NCH, D]), None]
        cols = sb("cols", [D, 12 + 16])
        rows = sb("rows", [D, 6, D])
        gl = sb("gelu", [D, 2, T])
        xhat = sb("xhat", [D, 2, D])
        ident = sb("ident", [D, D])
        lsel = sb("l_select", [D, 4, 32])
        bst = sb("bn_stats", [D, 2, 6])
        mv = sb("bn_mv", [D, 2, 2])
        rs = sb("rstd", [D, 2])
        rs0 = sb("var_eps", [D, 2])
        mhalf = sb("mhalf", [D, 2])
        qs = sb("quant_scalars", [D, 9, 16])

        early = ExitStack()
        W3 = [[sb("wqkv0_hi", [D, 3, 1024], F32R, early), sb("wqkv0_lo", [D, 3, 1024], F32R, early)]]
        early.close()
        Wf = [[sb("wp_hi", [D, 1024], F32R), sb("wp_lo", [D, 1024], F32R)]]
        L1hi = sb("l1w_hi", [D, 4, D], F32R)
        L1lo = sb("l1w_lo", [D, 4, D], F32R)
        hf1 = sb("h_full_l1", [D, NB, T])
        gT = sb("g_t", [D, NCH, T])
        L1 = sb("l1w", [D, 8, D])
        QKh = gT[:, 0:2, :].rearrange("p a b -> p (a b)").bitcast(F32R)
        QKl = gT[:, 2:4, :].rearrange("p a b -> p (a b)").bitcast(F32R)
        early = ExitStack()
        W3.append([sb("wqkv1_hi", [D, 3, 1024], F32R, early), sb("wqkv1_lo", [D, 3, 1024], F32R, early)])
        early.close()
        F1 = stage[:, 0, :]
        Wf.append([sb("ff1_hi", [D, 1024], F32R), sb("ff1_lo", [D, 1024], F32R)])
        W2[1] = sb("w2_1", [D, NCH, D])
        cf = sb("ctx_full", [C, NB * T])
        on = sb("o_norm", [D, 2, D])
        oT = sb("o_t", [D, T])
        r_dram = [nc.dram_tensor(f"r_scratch{i}", [H, T], F32).ap() for i in range(2)]
        qk_dram = [nc.dram_tensor(f"qk_scratch{i}", [2, D, 2 * T], F32).ap() for i in range(2)]
        pad_dram = nc.dram_tensor("pad_scratch", [2, 1, H, T], F32).ap()
        ps = [ctx.enter_context(nc.psum_tensor(f"bank{i}", [D, 512], F32)) for i in range(8)]
        SB, UB, LB, GB = ps[0:NS], ps[NS], ps[NS + 1], ps[NS + 2:8] + [ps[NS + 1]]

        g_ready = [sem(f"g_ready{i}") for i in range(NG + 1)]
        g_free = [sem(f"g_free{i}") for i in range(NG + 1)]
        hi_done = sem("hi_done")
        st_done = sem("st_done")
        exp_done = sem("exp_done")
        p_used = sem("p_used")
        u_ready, u_free = sem("u_ready"), sem("u_free")
        r_done = sem("r_done")
        r_put = sem("r_put")
        r_got = sem("r_got")
        norm_done = sem("norm_done")
        ln_stats, ln_rstd = sem("ln_stats"), sem("ln_rstd")
        ln_applied, xb_done = sem("ln_applied"), sem("xb_done")
        h_split = sem("h_split")
        m_row = [sem(f"max_rows{i}") for i in range(2)]
        q_copied = [sem(f"q_copied{m}") for m in range(4)]
        k_copied = [sem(f"k_copied{m}") for m in range(4)]
        consts = sem("consts")
        q_padded, k_padded = sem("q_padded"), sem("k_padded")
        loaded = [sem(f"loaded{i}") for i in range(5)]
        x_in_sem = sem("x_in")
        misc_in = sem("misc_in")
        wo_loaded = sem("wo_loaded")
        c_in = sem("c_in")
        c_split = sem("c_split")
        w_hi, w_lo = sem("w_hi"), sem("w_lo")
        qk_put = sem("qk_put")
        stacked = [[sem(f"stacked{i}{j}") for j in range(2)] for i in range(2)]
        zeroed = sem("zeroed")
        pad_put = sem("pad_put")
        padded = [sem(f"padded{i}") for i in range(3)]
        q_stats, q_all, q_scal, q_quant, q_split = (sem(n) for n in ("q_stats", "q_all", "q_scal", "q_quant", "q_split"))
        dve = sem("dve_chain")
        pool = sem("pool_chain")
        out_done = sem("out_done")

        hT_steps = [s for s in plan if s[0] == "hT"]
        ff1_steps = [s for s in plan if s[0] == "ff1"]

        def filled(eng, s):
            k, n = uses[s]
            eng.wait_ge(g_ready[k], n + 1)

        def emptied(eng, s):
            k, n = uses[s]
            eng.wait_ge(g_free[k], n + 1)

        def st_four(eng, u, m):
            eng.wait_ge(st_done, 16 * u + 4 * (m + 1))

        def st_half(eng, u, half):
            eng.wait_ge(st_done, 16 * u + 8 * (half + 1))

        def st_through(eng, u):
            eng.wait_ge(st_done, 16 * (u + 1))

        hi_count = {s: 0 for s in plan}
        run = 0
        for s in plan:
            if s[0] in ("q", "k", "hT", "ff1", "qk"):
                run += 2 if s[0] in ("q", "k") else 1
            hi_count[s] = run

        def u_index(u, p):
            return 8 * u + p if u < 8 else 64 + 4 * (u - 8) + p // 2

        def u_end(u):
            return 8 * (u + 1) if u < 8 else 64 + 4 * (u - 7)

        def unit_of(idx):
            return idx // 8 if idx < 64 else 8 + (idx - 64) // 4

        def released(eng, n):
            if n < 128:
                eng.wait_ge(p_used, n // 4 + 1)
            else:
                eng.wait_ge(u_ready, 64 + (n - 128) // 4 + 1)

        def wait_stacked(eng, u, half):
            k = half if ("stack", u, 0) in order else 1
            done = sum(1 for s in plan if s[0] == "stack" and s[1] <= u and (s[1] - u) % 2 == 0 and (s[2] > 0) == k)
            eng.wait_ge(stacked[u % 2][k], 128 * done)

        def kdim(a):
            return D if a % 2 == 0 else C

        def heads(m, odd):
            return slice(4 * m + odd, 4 * m + odd + 3, 2)

        ROWS = [slice(0, 64), slice(64, 128)]

        def view3(ap, n):
            return ap.rearrange("p (a b) -> p a b", a=n)

        block = ctx.enter_context(nc.Block())

        @block.sync
        def _(sp):
            def load_attn(a):
                for k in range(3):
                    r = D if k == 0 else kdim(a)
                    sp.dma_start(stage[0:r, k, :], w3_in[a][k]).then_inc(loaded[a], 16)

            sp.dma_start(x[:, 0:2, :], x_in[:, 0:2, :]).then_inc(x_in_sem, 16)
            load_attn(0)
            sp.dma_start(cols[:, :], cols_in).then_inc(misc_in, 16)
            sp.dma_start(rows[:, :, :], rows_in.partition_broadcast(D)).then_inc(misc_in, 16)
            sp.dma_start(x[:, 2:8, :], x_in[:, 2:8, :]).then_inc(misc_in, 16)
            sp.dma_start(R[0:C, 0:4, :].rearrange("p a b -> p (a b)"), ctx_in).then_inc(c_in, 16)
            for a in range(2):
                sp.dma_start(Wo[a][:, :, :], wo_in[a]).then_inc(wo_loaded, 16)
            for s in plan:
                name, u, i = s
                if name == "load":
                    if u == 1:
                        sp.wait_ge(w_lo, 3)
                        load_attn(1)
                    elif u == 2:
                        sp.wait_ge(w_lo, 6)
                        sp.dma_start(stage[:, 0, :], wp_in).then_inc(loaded[2], 16)
                        sp.dma_start(W2[0][:, :, :], w2_in).then_inc(loaded[2], 16)
                    elif u == 3:
                        filled(sp, ("k", 3, 3))
                        filled(sp, ("v", 3, 3))
                        sp.dma_start(L1[:, 0:FULL, :], l1_in[0]).then_inc(loaded[3], 16)
                        sp.dma_start(L1[0:C, FULL:8, :], l1_in[1]).then_inc(loaded[3], 16)
                    elif u == 4:
                        filled(sp, ("k", 7, 3))
                        filled(sp, ("v", 7, 3))
                        sp.wait_ge(w_lo, 7)
                        sp.dma_start(F1, ff1_in).then_inc(loaded[4], 16)
                        sp.dma_start(W2[1][:, :, :], ff2_in).then_inc(loaded[4], 16)
                        sp.dma_start(cf[:, :], ctx_in).then_inc(loaded[4], 16)
                elif name == "kpad":
                    sp.wait_ge(k_padded, 1)
                    for one in range(2):
                        for half in range(2):
                            sp.dma_start(pad_dram[one, :, 8 * half:8 * half + 8, :],
                                         K2[65 - one:66 - one, 0:H:2, :].bitcast(F32)).then_inc(pad_put, 16)
                elif name == "rcp":
                    sp.wait_ge(r_done, u + 1)
                    if u >= 2:
                        sp.wait_ge(r_got, 32 * (u - 1))
                    by_head = r_dram[u % 2].rearrange("(k c) i -> c k i", c=4)
                    for c in range(4):
                        sp.dma_start(by_head[c], Rc[32 * c:32 * c + 4, :]).then_inc(r_put, 16)
                elif name == "rread":
                    sp.wait_ge(r_put, 64 * (u + 1))
                    if u >= 1:
                        sp.wait_ge(norm_done, 2 * u)
                    else:
                        sp.wait_ge(c_split, 2)
                    by_side = r_dram[u % 2].rearrange("(p a) i -> a p i", a=2)
                    for a in range(2):
                        sp.dma_start(R[64 * a:64 * a + 64, :, :],
                                     by_side[a].partition_broadcast(64)).then_inc(r_got, 16)
                elif name in ("q", "k") and u < 8:
                    if u >= 1:
                        st_four(sp, u - 1, i)
                    for odd in range(2):
                        sp.wait_ge(hi_done, hi_count[s] - 1 + odd)
                        hs, own, other = heads(i, odd), ROWS[odd], ROWS[1 - odd]
                        if name == "q":
                            sp.dma_start(Q2[own, hs, :].bitcast(F32), Q1[own, hs, :].bitcast(F32)).then_inc(q_copied[i], 16)
                        else:
                            sp.dma_start(K1[other, hs, :].bitcast(F32), K1[own, hs, :].bitcast(F32)).then_inc(k_copied[i], 16)
                elif name == "mT":
                    emptied(sp, s)
                    if u < 8:
                        sp.wait_ge(q_padded, 1)
                        if u >= 1:
                            st_half(sp, u - 1, i)
                        dst = Q2
                    else:
                        if u >= 10:
                            st_half(sp, u - 2, i)
                        else:
                            st_half(sp, 7, i)
                        dst = QS[u % 2]
                    for odd in range(2):
                        row = (64, 0)[odd] if u < 8 else C
                        sp.dma_start(dst[row:row + 1, 8 * i + odd:8 * i + odd + 7:2, :].bitcast(F32),
                                     Mt[i][4 * odd:4 * odd + 4, :].bitcast(F32)).then_inc(m_row[i], 16)
                elif name == "qk":
                    emptied(sp, s)
                    if order[s] >= 2:
                        for half in range(2):
                            wait_stacked(sp, u - 2, half)
                    sp.dma_start(qk_dram[u % 2][0], QKh[:, :].bitcast(F32)).then_inc(qk_put, 16)
                    sp.dma_start(qk_dram[u % 2][1], QKl[:, :].bitcast(F32)).then_inc(qk_put, 16)
                elif name == "stack":
                    sp.wait_ge(qk_put, 32 * (order[("qk", u, 0)] + 1))
                    if i == 0:
                        st_half(sp, max(u - 2, 7), 0)
                    else:
                        st_through(sp, max(u - 2, 7))
                    hs = (slice(0, 8), slice(8, 16), slice(0, 16))[i]
                    if u in (8, 9):
                        sp.wait_ge(pad_put, 64)
                        sp.dma_start(KS[u % 2][32:C, hs, :].bitcast(F32),
                                     pad_dram[0][:, hs, :].partition_broadcast(C - 32)).then_inc(padded[i], 16)
                        sp.dma_start(KS[u % 2][C:C + 1, hs, :].bitcast(F32), pad_dram[1][:, hs, :]).then_inc(padded[i], 16)
                    sc = qk_dram[u % 2].rearrange("s (h d) i -> s d h i", d=DH1)
                    for t in range(4):
                        sp.dma_start(QS[u % 2][8 * t:8 * t + 8, hs, :].bitcast(F32), sc[t // 2][:, hs, 0:T])\
                          .then_inc(stacked[u % 2][i > 0], 16)
                        sp.dma_start(KS[u % 2][8 * t:8 * t + 8, hs, :].bitcast(F32), sc[t % 2][:, hs, T:2 * T])\
                          .then_inc(stacked[u % 2][i > 0], 16)
                elif name == "out":
                    emptied(sp, ("ff2", 4 + u, 0))
                    sp.dma_start(out[:, 2 * u:2 * u + 2, :], x[:, 2 * u:2 * u + 2, :]).then_inc(out_done, 16)
            sp.wait_ge(out_done, 16 * NB)

        @block.gpsimd
        def _(g):
            chain, zeroes, quantized = [0], [0], [0]

            def link(ins):
                ins.then_inc(pool, 1)
                chain[0] += 1
                g.wait_ge(pool, chain[0])

            link(g.memset(ident[:, :], 0.0))
            link(g.affine_select(out=ident[:, :], in_=ident[:, :], compare_op=ALU.not_equal, fill=1.0,
                                 base=0, pattern=[[-1, D]], channel_multiplier=1))
            link(g.memset(lsel[:, :, :], 1.0))
            link(g.memset(lsel[:, :, 0:4], 0.0))
            for k in range(4):
                link(g.memset(lsel[:, k, k:k + 1], 1.0))
            link(g.memset(qs[:, :, :], -3.0e38))
            g.memset(mhalf[:, :], -0.5).then_inc(consts, 1)
            g.wait_ge(consts, 1)

            def quantize(w, j):
                r, n = w.shape
                sc = lambda k: qs[0:r, k, j:j + 1]
                t = stage[0:r, 1, 0:n]
                link(g.tensor_scalar(t, w, sc(8), ROUND, ALU.mult, ALU.add))
                link(g.tensor_scalar(t, t, -ROUND, sc(3), ALU.add, ALU.max))
                link(g.tensor_scalar(t, t, sc(4), sc(2), ALU.min, ALU.mult))
                link(g.tensor_tensor(t, t, w, ALU.subtract))
                g.tensor_tensor(w, w, t, ALU.add).then_inc(q_quant, 1)
                g.wait_ge(q_quant, quantized[0] + 1)
                quantized[0] += 1

            for s in plan:
                name, u, i = s
                if name == "rread":
                    g.wait_ge(r_got, 32 * (u + 1))
                    g.wait_ge(u_free, u_end(u))
                    for half in range(2):
                        at = (8 * u + 4 * half) % RING
                        g.tensor_tensor(U[:, at:at + 4, :], U[:, at:at + 4, :],
                                        R[:, 4 * half:4 * half + 4, :], ALU.mult).then_inc(norm_done, 1)
                        g.wait_ge(norm_done, 2 * u + half + 1)
                elif name == "ln":
                    n = order[s]
                    g.wait_ge(ln_stats, n + 1)
                    link(g.tensor_scalar(rs0[:, :], mv[:, :, 1], EPS, None, ALU.add))
                    g.tensor_tensor(rs[:, :], rs0[:, :], mhalf[:, :], ALU.pow).then_inc(ln_rstd, 1)
                    g.wait_ge(ln_rstd, n + 1)
                elif name == "xh":
                    g.wait_ge(ln_applied, order[s] + 1)
                    if order[s] == 0:
                        g.wait_ge(misc_in, 48)
                    for t in range(2):
                        ins = g.tensor_tensor(x[:, 2 * i + t, :], x[:, 2 * i + t, :], rows[:, u, :], ALU.add)
                        if t == 0:
                            link(ins)
                    ins.then_inc(xb_done, 1)
                    g.wait_ge(xb_done, order[s] + 1)
                elif name == "kpad":
                    for odd in range(2):
                        rest, hs = ROWS[1 - odd], slice(odd, H, 2)
                        link(g.memset(K2[rest, hs, :].bitcast(F32), 0.0))
                        g.memset(K2[rest.start:rest.start + 1, hs, :].bitcast(F32), 1.0).then_inc(k_padded, 1)
                        g.wait_ge(k_padded, odd + 1)
                elif name == "qstat":
                    g.wait_ge(q_stats, u + 1)
                    g.partition_all_reduce(qs[:, 1, :], qs[:, 0, :], D, bass.bass_isa.ReduceOp.max).then_inc(q_all, 1)
                    g.wait_ge(q_all, u + 1)
                elif name == "qw":
                    g.wait_ge(q_scal, u + 1)
                    if u == 0:
                        quantize(L1[0:D if i < FULL else C, i, :], i)
                    elif i < 8:
                        quantize(F1[:, D * i:D * i + D], 0)
                    else:
                        quantize(W2[1][:, i - 8, :], 1)
                elif name == "v" and u in (8, 9):
                    if u == 8:
                        g.wait_ge(w_lo, 2)
                    else:
                        g.wait_ge(u_ready, u_end(7))
                    w = V1[u % 2]
                    link(g.memset(w[:, :, :, DH1:32], 0.0))
                    g.memset(w[:, :, :, DH1:DH1 + 1], 1.0).then_inc(zeroed, 1)
                    zeroes[0] += 1
                    g.wait_ge(zeroed, zeroes[0])

        @block.scalar
        def _(act):
            for s in plan:
                name, u, i = s
                if name in GENERAL:
                    bank = GB[uses[s][0]]
                    free = g_free[uses[s][0]]
                if name == "wsplit":
                    act.wait_ge(loaded[u], 48 if u < 2 else 32)
                    if u < 2:
                        rk = D if i == 0 else kdim(u)
                        dst, src = W3[u][0][0:rk, i, :], stage[0:rk, i, :]
                    else:
                        filled(act, ("k", 3, 3))
                        filled(act, ("v", 3, 3))
                        dst, src = Wf[0][0][:, :], stage[:, 0, :]
                    act.activation(dst, src, ACT.Copy).then_inc(w_hi, 1)
                elif name in ("q", "k"):
                    filled(act, s)
                    if u >= 1:
                        st_four(act, u - 1, i)
                    for odd in range(2):
                        act.activation((Q1 if name == "q" else K1)[ROWS[odd], heads(i, odd), :],
                                       view3(bank[ROWS[odd], :], 2), ACT.Copy).then_inc(hi_done, 1)
                elif name == "mT":
                    filled(act, s)
                    if u >= 1:
                        act.wait_ge(m_row[i], 32 * u)
                    act.activation(Mt[i][:, :], bank[0:8, 0:T], ACT.Copy).then_inc(free, 1)
                elif name == "v":
                    if u >= 8:
                        filled(act, s)
                        if u >= 9:
                            act.wait_ge(u_ready, u_end(u - 2))
                        for jc in range(2):
                            ins = act.activation(V1[u % 2][:, jc, :, 0:DH1],
                                                 bank[:, jc * D:jc * D + D].rearrange("p (h d) -> p h d", d=DH1), ACT.Copy)
                        ins.then_inc(free, 1)
                    elif i % 2 == 0:
                        filled(act, s)
                        if u >= 1:
                            act.wait_ge(u_ready, u_index(u - 1, 4 * (i // 2) + 3) + 1)
                        act.activation(V[:, i % 2, 512 * (i // 2):512 * (i // 2) + 512], bank[:, :], ACT.Copy)\
                           .then_inc(free, 1)
                elif name == "st":
                    n = order[s]
                    act.wait_ge(st_done, n + 1)
                    if n >= NP:
                        released(act, n - NP)
                    act.activation(Pr[n % NP][:, :], SB[n % NS][:, :], ACT.Exp,
                                   scale=float(DH0 if u < 8 else DH1) ** -0.5).then_inc(exp_done, 1)
                elif name == "pv":
                    n = u_index(u, i)
                    act.wait_ge(u_ready, n + 1)
                    if n >= RING:
                        w = unit_of(n - RING)
                        filled(act, ("wo", w, 0) if w < 8 else ("uT", w, 1))
                    act.activation(U[:, n % RING, :], UB[:, 0:T], ACT.Copy).then_inc(u_free, 1)
                elif name == "hT":
                    filled(act, s)
                    if order[s] == 0:
                        act.wait_ge(misc_in, 48)
                    act.activation(hh[:, i, :], bank[:, 0:T], ACT.Identity, bias=cols[:, 2 * u + 1:2 * u + 2],
                                   scale=cols[:, 2 * u:2 * u + 1]).then_inc(hi_done, 1)
                elif name == "ff1":
                    filled(act, s)
                    layer = u // 4
                    if order[s] >= 2:
                        emptied(act, ff1_steps[order[s] - 2])
                    bias = cols[:, 12 + 8 * layer + 4 + i:12 + 8 * layer + 5 + i]
                    act.activation(gl[:, i % 2, :], bank[:, 0:T], ACT.Gelu if layer == 0 else ACT.Gelu_apprx_tanh,
                                   bias=bias).then_inc(hi_done, 1)
                elif name == "qk":
                    filled(act, s)
                    if order[s] >= 1:
                        act.wait_ge(qk_put, 32 * order[s])
                    if order[s] < NB:
                        filled(act, ("ff2", order[s], 0))
                    act.activation(QKh[:, :], bank[:, :], ACT.Copy).then_inc(hi_done, 1)
                elif name == "oT":
                    filled(act, s)
                    if u > 8:
                        filled(act, ("wo", u - 1, 0))
                    act.activation(oT[:, :], bank[:, 0:T], ACT.Copy).then_inc(free, 1)

        @block.vector
        def _(v):
            chain = [0]

            def link(ins):
                ins.then_inc(dve, 1)
                chain[0] += 1
                v.wait_ge(dve, chain[0])

            for odd in range(2):
                ins = v.memset(Q2[ROWS[1 - odd], odd:H:2, :].bitcast(F32), 0.0)
            ins.then_inc(q_padded, 1)
            for s in plan:
                name, u, i = s
                if name in GENERAL:
                    bank = GB[uses[s][0]]
                    free = g_free[uses[s][0]]
                if name == "csplit":
                    v.wait_ge(c_in, 16)
                    raw = R[0:C, 0:4, :].rearrange("p a b -> p (a b)")
                    v.tensor_copy(chi[:, :], raw).then_inc(c_split, 1)
                    v.wait_ge(c_split, 1)
                    v.tensor_tensor(clo[:, :], raw, chi[:, :].bitcast(F32), ALU.subtract).then_inc(c_split, 1)
                elif name == "wsplit":
                    v.wait_ge(w_hi, order[s] + 1)
                    if u < 2:
                        rk = D if i == 0 else kdim(u)
                        dst, src = [W3[u][k][0:rk, i, :] for k in range(2)], stage[0:rk, i, :]
                    else:
                        dst, src = [Wf[0][k][:, :] for k in range(2)], stage[:, 0, :]
                    v.tensor_tensor(dst[1], src, dst[0].bitcast(F32), ALU.subtract).then_inc(w_lo, 1)
                elif name in ("q", "k"):
                    if u >= 1:
                        st_four(v, u - 1, i)
                    hi, lo = (Q1, Q1) if name == "q" else (K1, K2)
                    for odd in range(2):
                        v.wait_ge(hi_done, hi_count[s] - 1 + odd)
                        own = ROWS[odd]
                        to = ROWS[1 - odd] if name == "q" else own
                        hs = heads(i, odd)
                        ins = v.tensor_tensor(lo[to, hs, :], view3(bank[own, :], 2), hi[own, hs, :].bitcast(F32),
                                              ALU.subtract)
                    ins.then_inc(free, 1)
                elif name == "smax":
                    filled(v, s)
                    p, ic = i // 2, i % 2
                    if u >= 2:
                        filled(v, ("mT", u - 2, p // 4))
                    v.tensor_reduce(negm[u % 2][:, ic, p // 4, p % 4:p % 4 + 5:4], view3(bank[:, :], 2), AX.X, ALU.max,
                                    negate=True).then_inc(free, 1)
                elif name == "v":
                    if u < 8 and i % 2 == 1:
                        filled(v, s)
                        if u >= 1:
                            v.wait_ge(u_ready, u_index(u - 1, 4 * (i // 2) + 3) + 1)
                        v.tensor_copy(V[:, i % 2, 512 * (i // 2):512 * (i // 2) + 512], bank[:, :]).then_inc(free, 1)
                elif name == "rcp":
                    v.wait_ge(p_used, 4 * (u + 1))
                    if u >= 1:
                        v.wait_ge(r_put, 64 * u)
                    v.reciprocal(Rc[:, :], LB[:, 0:T]).then_inc(r_done, 1)
                elif name == "wo":
                    filled(v, s)
                    b = u % 4
                    v.wait_ge(xb_done, order[("xh", [0, 1, 3, 4][u // 4], b)] + 1)
                    v.tensor_tensor(x[:, 2 * b:2 * b + 2, :], view3(bank[:, 0:T], 2), x[:, 2 * b:2 * b + 2, :],
                                    ALU.add).then_inc(free, 1)
                elif name == "ff2":
                    filled(v, s)
                    b = u % 4
                    v.wait_ge(xb_done, order[("xh", 2 + 3 * (u // 4), b)] + 1)
                    v.tensor_tensor(x[:, 2 * b:2 * b + 2, :], view3(bank[:, 0:T], 2), x[:, 2 * b:2 * b + 2, :],
                                    ALU.add).then_inc(free, 1)
                elif name == "ln":
                    if u == 0:
                        v.wait_ge(x_in_sem, 16) if i == 0 else v.wait_ge(misc_in, 48)
                    elif u == 3:
                        emptied(v, ("ff2", i, 0))
                    else:
                        emptied(v, ("wo", {1: 0, 2: 4, 4: 8, 5: 12}[u] + i, 0))
                    n = order[s]
                    if n:
                        v.wait_ge(ln_applied, n)
                    for t in range(2):
                        ins = v.bn_stats(bst[:, t, :], x[:, 2 * i + t, :])
                        if t == 1:
                            link(ins)
                    v.bn_aggr(mv[:, 0, :], bst[:, 0, :])
                    v.bn_aggr(mv[:, 1, :], bst[:, 1, :]).then_inc(ln_stats, 1)
                elif name == "xh":
                    n = order[s]
                    v.wait_ge(ln_stats, n + 1)
                    v.wait_ge(ln_rstd, n + 1)
                    if n:
                        filled(v, hT_steps[n - 1])
                    for t in range(2):
                        ins = v.tensor_scalar(xhat[:, t, :], x[:, 2 * i + t, :], mv[:, t, 0:1], rs[:, t:t + 1],
                                              ALU.subtract, ALU.mult)
                    ins.then_inc(ln_applied, 1)
                elif name == "hT":
                    v.wait_ge(hi_done, hi_count[s])
                    n = order[s]
                    dst = hf1[:, i, :] if u == 3 else hf[:, n % 2, :]
                    if n:
                        v.wait_ge(h_split, n)
                    v.tensor_scalar(dst, bank[:, 0:T], cols[:, 2 * u:2 * u + 1], cols[:, 2 * u + 1:2 * u + 2],
                                    ALU.mult, ALU.add).then_inc(free, 1)
                    emptied(v, s)
                    v.tensor_tensor(hl[:, i, :], dst, hh[:, i, :].bitcast(F32), ALU.subtract).then_inc(h_split, 1)
                elif name == "ff1":
                    v.wait_ge(hi_done, hi_count[s])
                    layer = u // 4
                    if u >= 1:
                        filled(v, ("ff2", u - 1, 0))
                        v.wait_ge(qk_put, 32 * (u if u < NB else 2 * NB))
                    v.scalar_tensor_tensor(gT[:, i, :], bank[:, T:2 * T], cols[:, 12 + 8 * layer + i:13 + 8 * layer + i],
                                           gl[:, i % 2, :], ALU.add, ALU.mult).then_inc(free, 1)
                elif name == "qk":
                    v.wait_ge(hi_done, hi_count[s])
                    if order[s] >= 1:
                        v.wait_ge(qk_put, 32 * order[s])
                    if order[s] < NB:
                        filled(v, ("ff2", order[s], 0))
                    v.tensor_tensor(QKl[:, :], bank[:, :], QKh[:, :].bitcast(F32), ALU.subtract).then_inc(free, 1)
                elif name == "uT":
                    filled(v, s)
                    w = bank[:, :].rearrange("p (h r) -> p h r", r=32)
                    if u > 8:
                        filled(v, ("oT", u - 1, 0))
                    rec = qs[:, 5 + i, :]
                    link(v.reciprocal(rec, w[:, :, DH1]))
                    v.tensor_tensor(on[:, i, :].rearrange("p (h d) -> p h d", d=DH1), w[:, :, 0:DH1],
                                    rec.unsqueeze(2).to_broadcast([D, H, DH1]), ALU.mult).then_inc(free, 1)
                elif name == "qstat":
                    v.wait_ge(loaded[3 + u], 32 if u == 0 else 48)
                    if u == 0:
                        parts = [(slice(0, FULL), L1[:, 0:FULL, :], D), (slice(FULL, 8), L1[0:C, FULL:8, :], C)]
                    else:
                        parts = [(slice(0, 1), F1, D), (slice(1, 2), W2[1][:, :, :], D)]
                    for sl, w, r in parts:
                        ax = AX.XY if (u == 1 and sl.start == 1) else AX.X
                        for o, op, neg in ((0, ALU.max, False), (8, ALU.min, True)):
                            link(v.tensor_reduce(qs[0:r, 0, sl.start + o:sl.stop + o], w, ax, op, negate=neg))
                    v.tensor_copy(qs[:, 7, 8:9], qs[:, 0, 0:1]).then_inc(q_stats, 1)
                elif name == "qscal":
                    v.wait_ge(q_all, u + 1)
                    if u == 1:
                        v.wait_ge(q_quant, 8)
                    mx, mn = qs[:, 1, 0:8], qs[:, 1, 8:16]
                    link(v.tensor_tensor(qs[:, 2, 8:16], mx, mn, ALU.add))
                    link(v.tensor_scalar(qs[:, 2, 0:8], qs[:, 2, 8:16], 1.0 / LEVELS, None, ALU.mult))
                    link(v.reciprocal(qs[:, 8, 0:8], qs[:, 2, 0:8]))
                    link(v.tensor_tensor(qs[:, 3, 8:16], mn, qs[:, 8, 0:8], ALU.mult))
                    link(v.tensor_scalar(qs[:, 4, 8:16], qs[:, 3, 8:16], ROUND, None, ALU.add))
                    link(v.tensor_scalar(qs[:, 3, 0:8], qs[:, 4, 8:16], -ROUND, -1.0, ALU.add, ALU.mult))
                    v.tensor_scalar(qs[:, 4, 0:8], qs[:, 3, 0:8], LEVELS, None, ALU.add).then_inc(q_scal, 1)
                elif name == "qsplit":
                    v.wait_ge(q_quant, 8 if u == 0 else 20)
                    if u == 0:
                        for nm, k in SPLIT.items():
                            j = L1W.index(nm)
                            r = D if j < FULL else C
                            link(v.tensor_copy(L1hi[0:r, k, :], L1[0:r, j, :]))
                            ins = v.tensor_tensor(L1lo[0:r, k, :], L1[0:r, j, :], L1hi[0:r, k, :].bitcast(F32), ALU.subtract)
                    else:
                        link(v.tensor_copy(Wf[1][0][:, :], F1))
                        ins = v.tensor_tensor(Wf[1][1][:, :], F1, Wf[1][0][:, :].bitcast(F32), ALU.subtract)
                    ins.then_inc(q_split, 1)

        @block.tensor
        def _(pe):
            def claim(s):
                k, n = uses[s]
                if n:
                    pe.wait_ge(g_free[k], n)
                elif k == NG:
                    pe.wait_ge(r_done, 8)
                return GB[k]

            def three(dst, w, m, k, start=True, stop=True):
                pe.matmul(dst, w[0], m[0], start=start, stop=False, skip_group_check=True)
                pe.matmul(dst, w[1], m[0], start=False, stop=False, skip_group_check=True)
                return pe.matmul(dst, w[0], m[1], start=False, stop=stop, skip_group_check=True)

            pe.wait_ge(consts, 1)
            for s in plan:
                name, u, i = s
                if name in GENERAL:
                    bank = claim(s)
                    ready = g_ready[uses[s][0]]
                if name in ("q", "k"):
                    a, b = u // 4, u % 4
                    j = 0 if name == "q" else 1
                    of_ctx = a == 1 and name == "k"
                    pe.wait_ge(w_lo, order[("wsplit", a, j)] + 1)
                    if of_ctx:
                        pe.wait_ge(c_split, 2)
                        src = [chi[:, b * T:b * T + T], clo[:, b * T:b * T + T]]
                    else:
                        pe.wait_ge(h_split, order[("hT", a, b)] + 1)
                        src = [hh[:, b, :], hl[:, b, :]]
                    rk = C if of_ctx else D
                    for k in range(2):
                        at = D * (2 * i + k)
                        ins = three(bank[:, k * T:k * T + T], [W3[a][z][0:rk, j, at:at + D] for z in range(2)], src, rk)
                    ins.then_inc(ready, 1)
                elif name == "smax":
                    p, ic = i // 2, i % 2
                    if u < 8:
                        emptied(pe, ("q", u, p // 2))
                        emptied(pe, ("k", u, p // 2))
                        pe.wait_ge(k_copied[p // 2], 32 * (u + 1))
                        rk, q_of, k_of = D, Q1, K1
                    else:
                        wait_stacked(pe, u, p // 4)
                        if u in (8, 9):
                            pe.wait_ge(padded[p // 4 if u == 8 else 2], 32)
                        rk, q_of, k_of = C, QS[u % 2], KS[u % 2]
                    for j in range(2):
                        h = 2 * p + j
                        ins = pe.matmul(bank[:, j * T:j * T + T], q_of[0:rk, h, ic * D:ic * D + D], k_of[0:rk, h, :],
                                        start=True, stop=True)
                    ins.then_inc(ready, 1)
                elif name == "mT":
                    emptied(pe, ("smax", u, 8 * i + 7))
                    for ic in range(2):
                        ins = pe.transpose(bank[0:8, ic * D:ic * D + D], negm[u % 2][:, ic, i, :], ident[:, :])
                    ins.then_inc(ready, 1)
                elif name == "v":
                    b = u % 4
                    if u < 8:
                        a, dk, half, jc = u // 4, kdim(u // 4), i // 2, i % 2
                        pe.wait_ge(w_lo, order[("wsplit", a, 2)] + 1)
                        at = b * T + jc * D
                        if a == 0:
                            pe.wait_ge(h_split, order[("hT", 0, b)] + 1)
                            keys = [w[:, b, jc * D:jc * D + D] for w in (hh, hl)]
                        else:
                            pe.wait_ge(c_split, 2)
                            keys = [chi[:, at:at + D], clo[:, at:at + D]]
                        w = [W3[a][k][0:dk, 2, 512 * half:512 * half + 512] for k in range(2)]
                        ins = three(bank[:, :], keys, w, dk)
                    else:
                        pe.wait_ge(q_quant, 8)
                        j = L1W.index("v1" if u < 12 else "v2")
                        if u < 12:
                            pe.wait_ge(h_split, order[("hT", 3, b)] + 1)
                        else:
                            pe.wait_ge(loaded[4], 48)
                        for jc in range(2):
                            at = b * T + jc * D
                            keys = hf1[:, b, jc * D:jc * D + D] if u < 12 else cf[:, at:at + D]
                            ins = pe.matmul(bank[:, jc * D:jc * D + D], keys, L1[0:D if u < 12 else C, j, :],
                                            start=True, stop=True)
                    ins.then_inc(ready, 1)
                elif name == "st":
                    n, p, jc = order[s], i // 2, i % 2
                    if n >= NS:
                        pe.wait_ge(exp_done, n - NS + 1)
                    pe.wait_ge(m_row[p // 4], 32 * (u + 1))
                    bank = SB[n % NS]
                    if u < 8:
                        pe.wait_ge(k_padded, 2)
                        pe.wait_ge(q_padded, 1)
                        emptied(pe, ("q", u, p // 2))
                        emptied(pe, ("k", u, p // 2))
                        pe.wait_ge(k_copied[p // 2], 32 * (u + 1))
                        pe.wait_ge(q_copied[p // 2], 32 * (u + 1))
                        terms = [(K1, Q1, D), (K2, Q2, D)]
                    else:
                        terms = [(KS[u % 2], QS[u % 2], C + 1)]
                    for j in range(2):
                        h = 2 * p + j
                        for k, (k_of, q_of, rk) in enumerate(terms):
                            ins = pe.matmul(bank[:, j * T:j * T + T], k_of[0:rk, h, jc * D:jc * D + D], q_of[0:rk, h, :],
                                            start=(k == 0), stop=(k == len(terms) - 1))
                    ins.then_inc(st_done, 1)
                elif name == "pv":
                    n = u_index(u, i)
                    bank = UB
                    if n:
                        pe.wait_ge(u_free, n)
                    pe.wait_ge(exp_done, order[("st", u, 2 * i + 1)] + 1)
                    if u < 8:
                        emptied(pe, ("v", u, 2 * (i // 4)))
                        emptied(pe, ("v", u, 2 * (i // 4) + 1))
                        for jc in range(2):
                            pr = Pr[order[("st", u, 2 * i + jc)] % NP]
                            for j in range(2):
                                h = 2 * i + j
                                ins = pe.matmul(bank[64 * j:64 * j + 64, 0:T], V[:, jc, DH0 * h:DH0 * h + DH0],
                                                pr[:, j * T:j * T + T], start=(jc == 0), stop=(jc == 1))
                    else:
                        emptied(pe, ("v", u, 0))
                        pe.wait_ge(zeroed, 1 if u == 8 else 2)
                        for jc in range(2):
                            for c in range(4):
                                h = 4 * (i // 2) + c
                                pr = Pr[order[("st", u, 2 * (h // 2) + jc)] % NP]
                                ins = pe.matmul(bank[32 * c:32 * c + 32, 0:T], V1[u % 2][:, jc, h, :],
                                                pr[:, (h % 2) * T:(h % 2) * T + T], start=(jc == 0), stop=(jc == 1),
                                                tile_position=(0, 32 * c))
                    ins.then_inc(u_ready, 1)
                elif name == "L":
                    k = i // 2
                    if k == 0 and u >= 1:
                        pe.wait_ge(r_done, u)
                    for jc in range(2):
                        for c in range(4):
                            h = 4 * k + c
                            pr = Pr[order[("st", u, 2 * (h // 2) + jc)] % NP]
                            ins = pe.matmul(LB[32 * c:32 * c + 32, 0:T], lsel[:, k, :], pr[:, (h % 2) * T:(h % 2) * T + T],
                                            start=(k == 0 and jc == 0), stop=(k == 3 and jc == 1),
                                            tile_position=(0, 32 * c))
                    ins.then_inc(p_used, 1)
                elif name == "wo":
                    if u < 8:
                        pe.wait_ge(wo_loaded, 32)
                        pe.wait_ge(norm_done, 2 * (u + 1))
                        for t in range(2):
                            for p in range(PAIRS):
                                ins = pe.matmul(bank[:, t * D:t * D + D], U[:, (8 * u + p) % RING, t * D:t * D + D],
                                                Wo[u // 4][:, p, :], start=(p == 0), stop=(p == PAIRS - 1))
                    else:
                        emptied(pe, ("oT", u, 0))
                        j = L1W.index("o1" if u < 12 else "o2")
                        for t in range(2):
                            ins = pe.matmul(bank[:, t * D:t * D + D], oT[:, t * D:t * D + D], L1[:, j, :],
                                            start=True, stop=True)
                    ins.then_inc(ready, 1)
                elif name == "hT":
                    pe.wait_ge(ln_applied, order[s] + 1)
                    for t in range(2):
                        ins = pe.transpose(bank[:, t * D:t * D + D], xhat[:, t, :], ident[:, :])
                    ins.then_inc(ready, 1)
                elif name == "ff1":
                    layer, b = u // 4, u % 4
                    pe.wait_ge(h_split, order[("hT", 2 + 3 * layer, b)] + 1)
                    if layer == 0:
                        pe.wait_ge(w_lo, 7)
                    else:
                        pe.wait_ge(q_split, 2)
                    for half, ch in ((0, NCH + i), (1, i)):
                        ins = three(bank[:, half * T:half * T + T], [w[:, ch * D:ch * D + D] for w in Wf[layer]],
                                    [hh[:, b, :], hl[:, b, :]], D)
                    ins.then_inc(ready, 1)
                elif name == "ff2":
                    layer = u // 4
                    emptied(pe, ("ff1", u, NCH - 1))
                    if layer == 0:
                        pe.wait_ge(loaded[2], 32)
                    else:
                        pe.wait_ge(q_quant, 20)
                    for t in range(2):
                        for c in range(NCH):
                            ins = pe.matmul(bank[:, t * D:t * D + D], gT[:, c, t * D:t * D + D], W2[layer][:, c, :],
                                            start=(c == 0), stop=(c == NCH - 1))
                    ins.then_inc(ready, 1)
                elif name == "qk":
                    b, cross = u % 4, u >= 12
                    pe.wait_ge(q_split, 1)
                    pe.wait_ge(h_split, order[("hT", 4 if cross else 3, b)] + 1)
                    for half, nm in ((0, "q2" if cross else "q1"), (1, "k2" if cross else "k1")):
                        r = C if nm == "k2" else D
                        k = SPLIT[nm]
                        src = [chi[:, b * T:b * T + T], clo[:, b * T:b * T + T]] if nm == "k2" else [hh[:, b, :], hl[:, b, :]]
                        ins = three(bank[:, half * T:half * T + T], [L1hi[0:r, k, :], L1lo[0:r, k, :]], src, r)
                    ins.then_inc(ready, 1)
                elif name == "uT":
                    pe.wait_ge(u_free, u_end(u))
                    for g4 in range(4):
                        at = (64 + 4 * (u - 8) + g4) % RING
                        ins = pe.transpose(bank[:, g4 * D:g4 * D + D], U[:, at, i * D:i * D + D], ident[:, :])
                    ins.then_inc(ready, 1)
                elif name == "oT":
                    emptied(pe, ("uT", u, 0))
                    emptied(pe, ("uT", u, 1))
                    for t in range(2):
                        ins = pe.transpose(bank[:, t * D:t * D + D], on[:, t, :], ident[:, :])
                    ins.then_inc(ready, 1)


def kernel(**inputs):
    import concourse.bacc as bacc
    from concourse.bass_utils import run_bass_kernel_spmd

    a = {k: np.asarray(v) for k, v in inputs.items()}
    L0, L1n = "L0_xattn_", "L1_xattn_"
    flat = lambda w: np.ascontiguousarray(w)
    by_p = lambda w, n: flat(w.reshape(n, D, -1).transpose(1, 0, 2))
    arrays = {
        "x_tok": by_p(a["x"], 2 * NB),
        "ctx_t": flat(a["ctx_768"].reshape(NB * T, C).T),
        **{f"{w.lower()}{k}": a[f"{L0}{w}{k}"] for w in ("Wq", "Wk", "Wv") for k in (1, 2)},
        "wo1": by_p(a[L0 + "Wo1"], PAIRS), "wo2": by_p(a[L0 + "Wo2"], PAIRS),
        "wp": a[L0 + "Wp"], "w2": by_p(a[L0 + "W2"], NCH),
        "l1_full": flat(np.stack([a[f"{L1n}{n}_w"].T for n in L1W[:FULL]], 1)),
        "l1_ctx": flat(np.stack([a[f"{L1n}{n}_w"].T for n in L1W[FULL:]], 1)),
        "ff1_t": flat(a[L1n + "ff1_w"].T), "ff2_t": by_p(a[L1n + "ff2_w"].T, NCH),
        "cols": flat(np.concatenate([np.stack([
            a[L0 + "g1"], a[L0 + "be1"], a[L0 + "g2"], a[L0 + "be2"], a[L0 + "g3"], a[L0 + "be3"],
            a[L1n + "ln1_g"], a[L1n + "ln1_b"], a[L1n + "ln2_g"], a[L1n + "ln2_b"], a[L1n + "ln3_g"], a[L1n + "ln3_b"],
        ], 1), a[L0 + "bp"].reshape(8, D).T, a[L1n + "ff1_b"].reshape(8, D).T], 1)),
        "rows": flat(np.stack([a[L0 + "bo1"], a[L0 + "bo2"], a[L0 + "b2"],
                               a[L1n + "o1_b"], a[L1n + "o2_b"], a[L1n + "ff2_b"]], 0)),
    }
    nc = bacc.Bacc("TRN2", target_bir_lowering=False, num_devices=1)
    t = {n: nc.dram_tensor("in_" + n, w.shape, F32, kind="ExternalInput").ap() for n, w in arrays.items()}
    out = nc.dram_tensor("out", (D, 2 * NB, D), F32, kind="ExternalOutput").ap()
    build(nc, t["x_tok"], t["ctx_t"], [[t[f"{w}{k}"] for w in ("wq", "wk", "wv")] for k in (1, 2)],
          [t["wo1"], t["wo2"]], t["wp"], t["w2"], (t["l1_full"], t["l1_ctx"]), t["ff1_t"], t["ff2_t"],
          t["cols"], t["rows"], out)
    r = run_bass_kernel_spmd(nc, [{"in_" + n: w for n, w in arrays.items()}], core_ids=[0])
    got = r.results[0]["out"]
    return flat(got.transpose(1, 0, 2)).reshape(NB, T, D)
```

```python
from contextlib import ExitStack

import numpy as np

import concourse.bass as bass
from concourse import mybir

F32 = mybir.dt.float32
F32R = mybir.dt.float32r
ALU = mybir.AluOpType
ACT = mybir.ActivationFunctionType
AX = mybir.AxisListType

NB, T, D, C, H = 4, 256, 128, 96, 16
DH0, DH1 = 64, 8
NCH = 4
EPS = 1e-5
LEVELS = 255.0
ROUND = 12582912.0
NS, NG, NP, RING = 3, 3, 6, 12
UNITS = 4 * NB
PAIRS = H // 2
L1W = ["q1", "k1", "v1", "o1", "q2", "o2", "k2", "v2"]
FULL = 6
SPLIT = {"q1": 0, "k1": 1, "q2": 2, "k2": 3}


def make_plan():
    plan = []

    def merge(main, side):
        n = max(len(main), 1)
        items = [(8.0 * i / n, 0, i, s) for i, s in enumerate(main)]
        items += [(pos, 1, i, s) for i, (pos, s) in enumerate(side)]
        plan.extend(s for *_, s in sorted(items, key=lambda x: x[:3]))

    def attention_inputs(u, side):
        if u >= UNITS:
            return
        if u < 8:
            for m in range(4):
                side += [(0.45 + 2 * m, ("k", u, m)), (0.75 + 2 * m, ("q", u, m))]
            side += [(2 * (i // 4) + (2.1, 2.7, 3.4, 3.5)[i % 4], ("smax", u, i)) for i in range(12)]
            side.append((5.95, ("mT", u, 0)))
            side += [(4.3, ("v", u, 0)), (5.8, ("v", u, 1))]
        elif u == 8:
            side += [(4.4 + 0.15 * i, ("smax", u, i)) for i in range(8)]
            side.append((6.1, ("mT", u, 0)))
            side.append((2.0, ("v", u, 0)))
        else:
            first, step = {9: (2.3, 0.2), 10: (1.0, 0.38)}.get(u, (0.2, 0.43))
            side += [(first + step * i, ("smax", u, i)) for i in range(16)]
            side.append((max(4.3, first + step * 9), ("mT", u, 0)))
            side.append((7.9, ("mT", u, 1)))
            side.append((0.0, ("v", u, 0)))

    def rest_of_inputs(u, side):
        if u <= 8:
            if u < 8:
                side += [((0.1, 0.7, 1.2, 1.5)[i % 4], ("smax", u, i)) for i in range(12, 16)]
            else:
                side += [(1.0, ("smax", u, i)) for i in range(8, 16)]
            side.append((1.8 if u < 8 else 1.5, ("mT", u, 1)))
        if u < 8:
            side += [(0.4, ("v", u, 2)), (2.0, ("v", u, 3))]

    plan += [("ln", 0, 0), ("wsplit", 0, 1), ("xh", 0, 0), ("wsplit", 0, 0), ("hT", 0, 0), ("kpad", 0, 0)]
    plan += [("k", 0, 0), ("q", 0, 0), ("k", 0, 1), ("q", 0, 1), ("wsplit", 0, 2), ("ln", 0, 1), ("k", 0, 2), ("q", 0, 2)]
    plan += [("smax", 0, i) for i in range(4)] + [("xh", 0, 1), ("v", 0, 0)]
    plan += [("smax", 0, i) for i in range(4, 8)] + [("mT", 0, 0), ("hT", 0, 1), ("k", 0, 3), ("q", 0, 3), ("v", 0, 1)]
    plan += [("smax", 0, 8), ("smax", 0, 9), ("st", 0, 0), ("smax", 0, 10), ("st", 0, 1), ("smax", 0, 11)]

    for u in range(UNITS + 1):
        main, side = [], []
        if u < UNITS:
            for p in range(PAIRS):
                for jc in range(2):
                    if p + 1 < PAIRS:
                        main.append(("st", u, 2 * p + 2 + jc))
                    elif u + 1 < UNITS:
                        main.append(("st", u + 1, jc))
                if u < 8:
                    main.append(("pv", u, p))
                    if p % 2:
                        main.append(("L", u, p))
                elif p % 2:
                    main.append(("pv", u, p))
        if u < 2:
            side += [(2.2, ("ln", 0, u + 2)), (3.9, ("xh", 0, u + 2)), (4.6, ("hT", 0, u + 2))]
        rest_of_inputs(u, side)
        if u == 0:
            side += [(0.9, ("csplit", 0, 0)), (1.2, ("load", 1, 0))]
        if u == 1:
            side += [(1.2 + 2.0 * k, ("wsplit", 1, k)) for k in range(3)]
        if u == 2:
            side.append((2.0, ("load", 2, 0)))
        if u == 3:
            side += [(2.7, ("wsplit", 2, 0)), (2.6, ("load", 3, 0)), (6.3, ("qstat", 0, 0))]
        if u == 4:
            side.append((0.1, ("qscal", 0, 0)))
        if u in (4, 5):
            side += [((1.2, 1.6, 5.7, 7.0)[k], ("qw", 0, 4 * (u - 4) + k)) for k in range(4)]
        if u == 5:
            side.append((7.8, ("qsplit", 0, 0)))
        if u == 7:
            side.append((2.7, ("load", 4, 0)))
        if u == 9:
            side += [(0.2, ("qstat", 1, 0)), (3.8, ("qscal", 1, 0))]
        if u in (10, 11, 12):
            side += [((0.2, 1.4, 5.7, 7.0)[k], ("qw", 1, 4 * (u - 10) + k)) for k in range(4)]
        if u == 13:
            side.append((1.2, ("qsplit", 1, 0)))
        if 6 <= u <= 13:
            side.append((5.4 if u < 8 else 4.2 if u < 10 else 1.2, ("qk", u + 2, 0)))
        if u == 7:
            side += [(3.2, ("stack", 8, 0)), (6.6, ("stack", 8, 1)), (7.5, ("stack", 9, 2))]
        if 8 <= u <= 13:
            side.append((4.9 if u < 10 else 3.9, ("stack", u + 2, 0)))
        if 9 <= u <= 14:
            side.append((0.0, ("stack", u + 1, 1)))
        attention_inputs(u + 1, side)
        c = u - 1
        if 0 <= c < 8:
            side += [(0.3, ("rcp", c, 0)), (0.7, ("rread", c, 0)), (4.1, ("wo", c, 0))]
            k = 1 + c // 4
            side += [(4.2, ("ln", k, c % 4)), (5.7, ("xh", k, c % 4)), (6.4, ("hT", k, c % 4))]
        elif 8 <= c < UNITS:
            side += [(0.5, ("uT", c, 0)), (1.2, ("uT", c, 1)), (1.8, ("oT", c, 0)), (2.6, ("wo", c, 0))]
            k = 2 + c // 4
            at = 3.4 if u == 9 else 3.3
            side += [(at, ("ln", k, c % 4)), (at + 0.8, ("xh", k, c % 4)), (at + 2.0, ("hT", k, c % 4))]
        for layer, first, start in ((0, 6, 0.4), (1, 13, 6.1)):
            b = u - first
            if 0 <= b < NB:
                f = 4 * layer + b
                side += [(start + 0.01 * c4, ("ff1", f, c4)) for c4 in range(NCH)] + [(start + 1.4, ("ff2", f, 0))]
                if layer == 0:
                    at, gap = (1.9, 0.9) if u < 8 else (2.1, 0.7)
                    side += [(at, ("ln", 3, b)), (at + gap, ("xh", 3, b)), (at + 2 * gap, ("hT", 3, b))]
                else:
                    side.append((6.9, ("out", b, 0)))
        merge(main, side)
    return plan


GENERAL = {"q", "k", "smax", "mT", "v", "wo", "hT", "ff1", "ff2", "qk", "uT", "oT"}


def build(nc, x_in, ctx_in, w3_in, wo_in, wp_in, w2_in, l1_in, ff1_in, ff2_in, cols_in, rows_in, out):
    plan = make_plan()
    order, uses, n_of = {}, {}, {}
    in_bank, turn, banks = [0] * (NG + 1), 0, NG
    for s in plan:
        order[s] = n_of.get(s[0], 0)
        n_of[s[0]] = order[s] + 1
        if s[0] in GENERAL:
            k = turn % banks
            turn += 1
            uses[s] = (k, in_bank[k])
            in_bank[k] += 1
        elif s == ("rcp", 2 * NB - 1, 0):
            banks, turn = NG + 1, NG

    ctx = ExitStack()
    with ctx:
        def sb(name, shape, dt=F32, scope=ctx):
            return scope.enter_context(nc.sbuf_tensor(name, shape, dt))

        def sem(name):
            return ctx.enter_context(nc.semaphore(name))

        x = sb("x", [D, 2 * NB, D])
        hh = sb("h_hi", [D, NB, T], F32R)
        hl = sb("h_lo", [D, NB, T], F32R)
        hf = sb("h_full", [D, 2, T])
        chi = sb("ctx_hi", [C, NB * T], F32R)
        clo = sb("ctx_lo", [C, NB * T], F32R)
        Q1, Q2, K1, K2 = (sb(n, [D, H, T], F32R) for n in ("q_hi_lo", "q_hi_max", "k_hi_hi", "k_lo_one"))
        QS, KS = [Q1, Q2], [K1, K2]
        V = sb("v", [D, 2, H * DH0])
        Pr = [sb(f"p{i}", [D, 2 * T]) for i in range(NP)]
        U = sb("u", [D, RING, T])
        R = sb("r", [D, PAIRS, T])
        Rc = sb("r_rows", [D, T])
        Wo = [sb(f"wo{a}", [D, PAIRS, D]) for a in range(2)]
        stage = sb("stage", [D, 3, 1024])
        V1 = [w.rearrange("p (j h r) -> p j h r", j=2, h=H) for w in (stage[:, 2, :], V[:, 0, :])]
        Mt = [sb(f"m{i}", [8, T], F32R) for i in range(2)]
        negm = [sb(f"negmax{i}", [D, 2, 2, 8]) for i in range(2)]
        W2 = [sb("w2_0", [D, NCH, D]), None]
        cols = sb("cols", [D, 12 + 16])
        rows = sb("rows", [D, 6, D])
        gl = sb("gelu", [D, 2, T])
        xhat = sb("xhat", [D, 2, D])
        ident = sb("ident", [D, D])
        lsel = sb("l_select", [D, 4, 32])
        bst = sb("bn_stats", [D, 2, 6])
        mv = sb("bn_mv", [D, 2, 2])
        rs = sb("rstd", [D, 2])
        rs0 = sb("var_eps", [D, 2])
        mhalf = sb("mhalf", [D, 2])
        qs = sb("quant_scalars", [D, 9, 16])

        early = ExitStack()
        W3 = [[sb("wqkv0_hi", [D, 3, 1024], F32R, early), sb("wqkv0_lo", [D, 3, 1024], F32R, early)]]
        early.close()
        Wf = [[sb("wp_hi", [D, 1024], F32R), sb("wp_lo", [D, 1024], F32R)]]
        L1hi = sb("l1w_hi", [D, 4, D], F32R)
        L1lo = sb("l1w_lo", [D, 4, D], F32R)
        hf1 = sb("h_full_l1", [D, NB, T])
        gT = sb("g_t", [D, NCH, T])
        L1 = sb("l1w", [D, 8, D])
        QKh = gT[:, 0:2, :].rearrange("p a b -> p (a b)").bitcast(F32R)
        QKl = gT[:, 2:4, :].rearrange("p a b -> p (a b)").bitcast(F32R)
        early = ExitStack()
        W3.append([sb("wqkv1_hi", [D, 3, 1024], F32R, early), sb("wqkv1_lo", [D, 3, 1024], F32R, early)])
        early.close()
        F1 = stage[:, 0, :]
        Wf.append([sb("ff1_hi", [D, 1024], F32R), sb("ff1_lo", [D, 1024], F32R)])
        W2[1] = sb("w2_1", [D, NCH, D])
        cf = sb("ctx_full", [C, NB * T])
        on = sb("o_norm", [D, 2, D])
        oT = sb("o_t", [D, T])
        r_dram = [nc.dram_tensor(f"r_scratch{i}", [H, T], F32).ap() for i in range(2)]
        qk_dram = [nc.dram_tensor(f"qk_scratch{i}", [2, 2, DH1, H, T], F32).ap() for i in range(2)]
        pad_dram = nc.dram_tensor("pad_scratch", [2, 1, H, T], F32).ap()
        ps = [ctx.enter_context(nc.psum_tensor(f"bank{i}", [D, 512], F32)) for i in range(8)]
        SB, UB, LB, GB = ps[0:NS], ps[NS], ps[NS + 1], ps[NS + 2:8] + [ps[NS + 1]]

        g_ready = [sem(f"g_ready{i}") for i in range(NG + 1)]
        g_free = [sem(f"g_free{i}") for i in range(NG + 1)]
        hi_done = sem("hi_done")
        st_done = sem("st_done")
        exp_done = sem("exp_done")
        p_used = sem("p_used")
        u_ready, u_free = sem("u_ready"), sem("u_free")
        r_done = sem("r_done")
        r_put, r_got = sem("r_put"), sem("r_got")
        norm_done = sem("norm_done")
        ln_stats, ln_rstd = sem("ln_stats"), sem("ln_rstd")
        ln_applied, xb_done = sem("ln_applied"), sem("xb_done")
        h_split = sem("h_split")
        m_row = [sem(f"max_rows{i}") for i in range(2)]
        q_copied = [sem(f"q_copied{m}") for m in range(4)]
        k_copied = [sem(f"k_copied{m}") for m in range(4)]
        consts = sem("consts")
        q_padded, k_padded = sem("q_padded"), sem("k_padded")
        loaded = [sem(f"loaded{i}") for i in range(5)]
        w3_loaded = [sem(f"w{n}_loaded") for n in "qkv"]
        x_in_sem = sem("x_in")
        misc_in = sem("misc_in")
        cols_loaded = sem("cols_loaded")
        wo_loaded = sem("wo_loaded")
        c_in = sem("c_in")
        c_split = sem("c_split")
        w_hi, w_lo = sem("w_hi"), [sem("w_lo_dve"), sem("w_lo_pool")]
        qk_put = sem("qk_put")
        stacked = [[sem(f"stacked{i}{j}") for j in range(2)] for i in range(2)]
        zeroed = sem("zeroed")
        pad_put = sem("pad_put")
        padded = [sem(f"padded{i}") for i in range(3)]
        q_stats, q_all, q_scal, q_quant, q_split = (sem(n) for n in ("q_stats", "q_all", "q_scal", "q_quant", "q_split"))
        dve = sem("dve_chain")
        pool = sem("pool_chain")
        out_done = sem("out_done")

        hT_steps = [s for s in plan if s[0] == "hT"]
        ff1_steps = [s for s in plan if s[0] == "ff1"]

        def filled(eng, s):
            k, n = uses[s]
            eng.wait_ge(g_ready[k], n + 1)

        def emptied(eng, s):
            k, n = uses[s]
            eng.wait_ge(g_free[k], n + 1)

        def st_four(eng, u, m):
            eng.wait_ge(st_done, 16 * u + 4 * (m + 1))

        def st_half(eng, u, half):
            eng.wait_ge(st_done, 16 * u + 8 * (half + 1))

        def st_through(eng, u):
            eng.wait_ge(st_done, 16 * (u + 1))

        hi_count = {s: 0 for s in plan}
        run = 0
        for s in plan:
            if s[0] in ("q", "k", "hT", "ff1", "qk"):
                run += 2 if s[0] in ("q", "k") else 1
            hi_count[s] = run

        def u_index(u, p):
            return 8 * u + p if u < 8 else 64 + 4 * (u - 8) + p // 2

        def u_end(u):
            return 8 * (u + 1) if u < 8 else 64 + 4 * (u - 7)

        def unit_of(idx):
            return idx // 8 if idx < 64 else 8 + (idx - 64) // 4

        def released(eng, n):
            if n < 128:
                eng.wait_ge(p_used, n // 4 + 1)
            else:
                eng.wait_ge(u_ready, 64 + (n - 128) // 4 + 1)

        def wait_stacked(eng, u, half):
            k = half if ("stack", u, 0) in order else 1
            done = sum(1 for s in plan if s[0] == "stack" and s[1] <= u and (s[1] - u) % 2 == 0 and (s[2] > 0) == k)
            eng.wait_ge(stacked[u % 2][k], 64 * done)

        def kdim(a):
            return D if a % 2 == 0 else C

        def heads(m, odd):
            return slice(4 * m + odd, 4 * m + odd + 3, 2)

        ROWS = [slice(0, 64), slice(64, 128)]

        def view3(ap, n):
            return ap.rearrange("p (a b) -> p a b", a=n)

        def split_weight(eng, s):
            _, a, i = s
            eng.wait_ge(w_hi, order[s] + 1)
            if a < 2:
                r = D if i == 0 else kdim(a)
                hi, lo = (W3[a][k][0:r, i, :] for k in range(2))
                src = stage[0:r, i, :]
            else:
                hi, lo, src = Wf[0][0][:, :], Wf[0][1][:, :], stage[:, 0, :]
            eng.tensor_tensor(lo, src, hi.bitcast(F32), ALU.subtract).then_inc(w_lo[a > 0], 1)

        def split_done(eng, s):
            eng.wait_ge(w_lo[s[1] > 0], order[s] + 1 - 3 * (s[1] > 0))

        block = ctx.enter_context(nc.Block())

        @block.sync
        def _(sp):
            def load_attn(a):
                for k in (1, 0, 2):
                    r = D if k == 0 else kdim(a)
                    sp.dma_start(stage[0:r, k, :], w3_in[a][k]).then_inc(w3_loaded[k], 16)

            sp.dma_start(x[:, 0:2, :], x_in[:, 0:2, :]).then_inc(x_in_sem, 16)
            sp.dma_start(cols[:, :], cols_in).then_inc(cols_loaded, 16)
            load_attn(0)
            sp.dma_start(rows[:, :, :], rows_in.partition_broadcast(D)).then_inc(misc_in, 16)
            sp.dma_start(x[:, 2:8, :], x_in[:, 2:8, :]).then_inc(misc_in, 16)
            sp.dma_start(R[0:C, 0:4, :].rearrange("p a b -> p (a b)"), ctx_in).then_inc(c_in, 16)
            for a in range(2):
                sp.dma_start(Wo[a][:, :, :], wo_in[a]).then_inc(wo_loaded, 16)
            for s in plan:
                name, u, i = s
                if name == "load":
                    if u == 1:
                        sp.wait_ge(w_lo[0], 3)
                        load_attn(1)
                    elif u == 2:
                        sp.wait_ge(w_lo[1], 3)
                        sp.dma_start(stage[:, 0, :], wp_in).then_inc(loaded[2], 16)
                        sp.dma_start(W2[0][:, :, :], w2_in).then_inc(loaded[2], 16)
                    elif u == 3:
                        filled(sp, ("k", 3, 3))
                        filled(sp, ("v", 3, 3))
                        sp.dma_start(L1[:, 0:FULL, :], l1_in[0]).then_inc(loaded[3], 16)
                        sp.dma_start(L1[0:C, FULL:8, :], l1_in[1]).then_inc(loaded[3], 16)
                    elif u == 4:
                        filled(sp, ("k", 7, 3))
                        filled(sp, ("v", 7, 3))
                        sp.wait_ge(w_lo[1], 4)
                        sp.dma_start(F1, ff1_in).then_inc(loaded[4], 16)
                        sp.dma_start(W2[1][:, :, :], ff2_in).then_inc(loaded[4], 16)
                        sp.dma_start(cf[:, :], ctx_in).then_inc(loaded[4], 16)
                elif name == "kpad":
                    sp.wait_ge(k_padded, 1)
                    for one in range(2):
                        for half in range(2):
                            sp.dma_start(pad_dram[one, :, 8 * half:8 * half + 8, :],
                                         K2[65 - one:66 - one, 0:H:2, :].bitcast(F32)).then_inc(pad_put, 16)
                elif name == "rcp":
                    sp.wait_ge(r_done, u + 1)
                    if u >= 2:
                        sp.wait_ge(r_got, 32 * (u - 1))
                    by_head = r_dram[u % 2].rearrange("(k c) i -> c k i", c=4)
                    for c in range(4):
                        sp.dma_start(by_head[c], Rc[32 * c:32 * c + 4, :]).then_inc(r_put, 16)
                elif name == "rread":
                    sp.wait_ge(r_put, 64 * (u + 1))
                    if u >= 1:
                        sp.wait_ge(norm_done, 2 * u)
                    else:
                        sp.wait_ge(c_split, 2)
                    by_side = r_dram[u % 2].rearrange("(p a) i -> a p i", a=2)
                    for a in range(2):
                        sp.dma_start(R[64 * a:64 * a + 64, :, :],
                                     by_side[a].partition_broadcast(64)).then_inc(r_got, 16)
                elif name in ("q", "k") and u < 8:
                    if u >= 1:
                        st_four(sp, u - 1, i)
                    for odd in range(2):
                        sp.wait_ge(hi_done, hi_count[s] - 1 + odd)
                        hs, own, other = heads(i, odd), ROWS[odd], ROWS[1 - odd]
                        if name == "q":
                            sp.dma_start(Q2[own, hs, :].bitcast(F32), Q1[own, hs, :].bitcast(F32)).then_inc(q_copied[i], 16)
                        else:
                            sp.dma_start(K1[other, hs, :].bitcast(F32), K1[own, hs, :].bitcast(F32)).then_inc(k_copied[i], 16)
                elif name == "mT":
                    emptied(sp, s)
                    sp.wait_ge(q_padded, 1)
                    if u >= 1:
                        st_half(sp, u - 1 if u < 8 else max(u - 2, 7), i)
                    dst = Q2 if u < 8 else QS[u % 2]
                    for odd in range(2):
                        row = (64, 0)[odd] if u < 8 else C
                        sp.dma_start(dst[row:row + 1, 8 * i + odd:8 * i + odd + 7:2, :].bitcast(F32),
                                     Mt[i][4 * odd:4 * odd + 4, :].bitcast(F32)).then_inc(m_row[i], 16)
                elif name == "qk":
                    emptied(sp, s)
                    if order[s] >= 2:
                        for half in range(2):
                            wait_stacked(sp, u - 2, half)
                    for w in range(2):
                        for s_, part in enumerate((QKh, QKl)):
                            sp.dma_start(qk_dram[u % 2][w, s_].rearrange("d h i -> h d i"),
                                         part[:, w * T:w * T + T].bitcast(F32)).then_inc(qk_put, 16)
                elif name == "stack":
                    sp.wait_ge(qk_put, 64 * (order[("qk", u, 0)] + 1))
                    if i == 0:
                        st_half(sp, max(u - 2, 7), 0)
                    else:
                        st_through(sp, max(u - 2, 7))
                    hs = (slice(0, 8), slice(8, 16), slice(0, 16))[i]
                    if u in (8, 9):
                        sp.wait_ge(pad_put, 64)
                        sp.dma_start(KS[u % 2][32:C, hs, :].bitcast(F32),
                                     pad_dram[0][:, hs, :].partition_broadcast(C - 32)).then_inc(padded[i], 16)
                        sp.dma_start(KS[u % 2][C:C + 1, hs, :].bitcast(F32), pad_dram[1][:, hs, :]).then_inc(padded[i], 16)
                    for t in range(2):
                        q16, k16 = (w[u % 2][16 * t:16 * t + 16, hs, :].bitcast(F32)
                                    .rearrange("p h i -> p (h i)") for w in (QS, KS))
                        part = qk_dram[u % 2][0, t, :, hs, :].rearrange("d h i -> d (h i)")
                        sp.dma_start(q16, part.unsqueeze(0).to_broadcast([2, DH1, part.shape[1]]))\
                          .then_inc(stacked[u % 2][i > 0], 16)
                        sp.dma_start(k16, qk_dram[u % 2][1, :, :, hs, :].rearrange("s d h i -> s d (h i)"))\
                          .then_inc(stacked[u % 2][i > 0], 16)
                elif name == "out":
                    emptied(sp, ("ff2", 4 + u, 0))
                    sp.dma_start(out[:, 2 * u:2 * u + 2, :], x[:, 2 * u:2 * u + 2, :]).then_inc(out_done, 16)
            sp.wait_ge(out_done, 16 * NB)

        @block.gpsimd
        def _(g):
            chain, zeroes, quantized = [0], [0], [0]

            def link(ins):
                ins.then_inc(pool, 1)
                chain[0] += 1
                g.wait_ge(pool, chain[0])

            link(g.memset(ident[:, :], 0.0))
            link(g.affine_select(out=ident[:, :], in_=ident[:, :], compare_op=ALU.not_equal, fill=1.0,
                                 base=0, pattern=[[-1, D]], channel_multiplier=1))
            link(g.memset(lsel[:, :, :], 1.0))
            link(g.memset(lsel[:, :, 0:4], 0.0))
            for k in range(4):
                link(g.memset(lsel[:, k, k:k + 1], 1.0))
            link(g.memset(qs[:, :, :], -3.0e38))
            g.memset(mhalf[:, :], -0.5).then_inc(consts, 1)
            g.wait_ge(consts, 1)

            def quantize(w, j):
                r, n = w.shape
                sc = lambda k: qs[0:r, k, j:j + 1]
                t = stage[0:r, 1, 0:n]
                link(g.tensor_scalar(t, w, sc(8), ROUND, ALU.mult, ALU.add))
                link(g.tensor_scalar(t, t, -ROUND, sc(3), ALU.add, ALU.max))
                link(g.tensor_scalar(t, t, sc(4), sc(2), ALU.min, ALU.mult))
                link(g.tensor_tensor(t, t, w, ALU.subtract))
                g.tensor_tensor(w, w, t, ALU.add).then_inc(q_quant, 1)
                g.wait_ge(q_quant, quantized[0] + 1)
                quantized[0] += 1

            for s in plan:
                name, u, i = s
                if name == "wsplit" and u > 0:
                    split_weight(g, s)
                    split_done(g, s)
                elif name == "rread":
                    g.wait_ge(r_got, 32 * (u + 1))
                    g.wait_ge(u_free, u_end(u))
                    for half in range(2):
                        at = (8 * u + 4 * half) % RING
                        g.tensor_tensor(U[:, at:at + 4, :], U[:, at:at + 4, :],
                                        R[:, 4 * half:4 * half + 4, :], ALU.mult).then_inc(norm_done, 1)
                        g.wait_ge(norm_done, 2 * u + half + 1)
                elif name == "ln":
                    n = order[s]
                    g.wait_ge(ln_stats, n + 1)
                    link(g.tensor_scalar(rs0[:, :], mv[:, :, 1], EPS, None, ALU.add))
                    g.tensor_tensor(rs[:, :], rs0[:, :], mhalf[:, :], ALU.pow).then_inc(ln_rstd, 1)
                    g.wait_ge(ln_rstd, n + 1)
                elif name == "xh":
                    g.wait_ge(ln_applied, order[s] + 1)
                    if order[s] == 0:
                        g.wait_ge(misc_in, 32)
                    for t in range(2):
                        ins = g.tensor_tensor(x[:, 2 * i + t, :], x[:, 2 * i + t, :], rows[:, u, :], ALU.add)
                        if t == 0:
                            link(ins)
                    ins.then_inc(xb_done, 1)
                    g.wait_ge(xb_done, order[s] + 1)
                elif name == "kpad":
                    for odd in range(2):
                        rest, hs = ROWS[1 - odd], slice(odd, H, 2)
                        link(g.memset(K2[rest, hs, :].bitcast(F32), 0.0))
                        g.memset(K2[rest.start:rest.start + 1, hs, :].bitcast(F32), 1.0).then_inc(k_padded, 1)
                        g.wait_ge(k_padded, odd + 1)
                elif name == "qstat":
                    g.wait_ge(q_stats, u + 1)
                    g.partition_all_reduce(qs[:, 1, :], qs[:, 0, :], D, bass.bass_isa.ReduceOp.max).then_inc(q_all, 1)
                    g.wait_ge(q_all, u + 1)
                elif name == "qw":
                    g.wait_ge(q_scal, u + 1)
                    if u == 0:
                        quantize(L1[0:D if i < FULL else C, i, :], i)
                    elif i < 8:
                        quantize(F1[:, D * i:D * i + D], 0)
                    else:
                        quantize(W2[1][:, i - 8, :], 1)
                elif name == "v" and u in (8, 9):
                    if u == 8:
                        g.wait_ge(w_lo[1], 3)
                    else:
                        g.wait_ge(u_ready, u_end(7))
                    w = V1[u % 2]
                    link(g.memset(w[:, :, :, DH1:32], 0.0))
                    g.memset(w[:, :, :, DH1:DH1 + 1], 1.0).then_inc(zeroed, 1)
                    zeroes[0] += 1
                    g.wait_ge(zeroed, zeroes[0])

        @block.scalar
        def _(act):
            for s in plan:
                name, u, i = s
                if name in GENERAL:
                    bank = GB[uses[s][0]]
                    free = g_free[uses[s][0]]
                if name == "wsplit":
                    if u == 2:
                        act.wait_ge(loaded[2], 32)
                    else:
                        act.wait_ge(w3_loaded[i], 16 * (u + 1))
                    if u < 2:
                        rk = D if i == 0 else kdim(u)
                        dst, src = W3[u][0][0:rk, i, :], stage[0:rk, i, :]
                    else:
                        filled(act, ("k", 3, 3))
                        filled(act, ("v", 3, 3))
                        dst, src = Wf[0][0][:, :], stage[:, 0, :]
                    act.activation(dst, src, ACT.Copy).then_inc(w_hi, 1)
                elif name in ("q", "k"):
                    filled(act, s)
                    if u >= 1:
                        st_four(act, u - 1, i)
                    for odd in range(2):
                        act.activation((Q1 if name == "q" else K1)[ROWS[odd], heads(i, odd), :],
                                       view3(bank[ROWS[odd], :], 2), ACT.Copy).then_inc(hi_done, 1)
                elif name == "mT":
                    filled(act, s)
                    if u >= 1:
                        act.wait_ge(m_row[i], 32 * u)
                    act.activation(Mt[i][:, :], bank[0:8, 0:T], ACT.Copy).then_inc(free, 1)
                elif name == "v":
                    if u >= 8:
                        filled(act, s)
                        if u >= 9:
                            act.wait_ge(u_ready, u_end(u - 2))
                        for jc in range(2):
                            ins = act.activation(V1[u % 2][:, jc, :, 0:DH1],
                                                 bank[:, jc * D:jc * D + D].rearrange("p (h d) -> p h d", d=DH1), ACT.Copy)
                        ins.then_inc(free, 1)
                    elif i % 2 == 0:
                        filled(act, s)
                        if u >= 1:
                            act.wait_ge(u_ready, u_index(u - 1, 4 * (i // 2) + 3) + 1)
                        act.activation(V[:, i % 2, 512 * (i // 2):512 * (i // 2) + 512], bank[:, :], ACT.Copy)\
                           .then_inc(free, 1)
                elif name == "st":
                    n = order[s]
                    act.wait_ge(st_done, n + 1)
                    if n >= NP:
                        released(act, n - NP)
                    act.activation(Pr[n % NP][:, :], SB[n % NS][:, :], ACT.Exp,
                                   scale=float(DH0 if u < 8 else DH1) ** -0.5).then_inc(exp_done, 1)
                elif name == "pv":
                    n = u_index(u, i)
                    act.wait_ge(u_ready, n + 1)
                    if n >= RING:
                        w = unit_of(n - RING)
                        filled(act, ("wo", w, 0) if w < 8 else ("uT", w, 1))
                    act.activation(U[:, n % RING, :], UB[:, 0:T], ACT.Copy).then_inc(u_free, 1)
                elif name == "hT":
                    filled(act, s)
                    if order[s] == 0:
                        act.wait_ge(cols_loaded, 16)
                    act.activation(hh[:, i, :], bank[:, 0:T], ACT.Identity, bias=cols[:, 2 * u + 1:2 * u + 2],
                                   scale=cols[:, 2 * u:2 * u + 1]).then_inc(hi_done, 1)
                elif name == "ff1":
                    filled(act, s)
                    layer = u // 4
                    if order[s] >= 2:
                        emptied(act, ff1_steps[order[s] - 2])
                    bias = cols[:, 12 + 8 * layer + 4 + i:12 + 8 * layer + 5 + i]
                    act.activation(gl[:, i % 2, :], bank[:, 0:T], ACT.Gelu if layer == 0 else ACT.Gelu_apprx_tanh,
                                   bias=bias).then_inc(hi_done, 1)
                elif name == "qk":
                    filled(act, s)
                    if order[s] >= 1:
                        act.wait_ge(qk_put, 64 * order[s])
                    if order[s] < NB:
                        filled(act, ("ff2", order[s], 0))
                    act.activation(QKh[:, :], bank[:, :], ACT.Copy).then_inc(hi_done, 1)
                elif name == "oT":
                    filled(act, s)
                    if u > 8:
                        filled(act, ("wo", u - 1, 0))
                    act.activation(oT[:, :], bank[:, 0:T], ACT.Copy).then_inc(free, 1)

        @block.vector
        def _(v):
            chain = [0]

            def link(ins):
                ins.then_inc(dve, 1)
                chain[0] += 1
                v.wait_ge(dve, chain[0])

            for odd in range(2):
                ins = v.memset(Q2[ROWS[1 - odd], odd:H:2, :].bitcast(F32), 0.0)
            ins.then_inc(q_padded, 1)
            for s in plan:
                name, u, i = s
                if name in GENERAL:
                    bank = GB[uses[s][0]]
                    free = g_free[uses[s][0]]
                if name == "csplit":
                    v.wait_ge(c_in, 16)
                    raw = R[0:C, 0:4, :].rearrange("p a b -> p (a b)")
                    v.tensor_copy(chi[:, :], raw).then_inc(c_split, 1)
                    v.wait_ge(c_split, 1)
                    v.tensor_tensor(clo[:, :], raw, chi[:, :].bitcast(F32), ALU.subtract).then_inc(c_split, 1)
                elif name == "wsplit" and u == 0:
                    split_weight(v, s)
                elif name in ("q", "k"):
                    if u >= 1:
                        st_four(v, u - 1, i)
                    hi, lo = (Q1, Q1) if name == "q" else (K1, K2)
                    for odd in range(2):
                        v.wait_ge(hi_done, hi_count[s] - 1 + odd)
                        own = ROWS[odd]
                        to = ROWS[1 - odd] if name == "q" else own
                        hs = heads(i, odd)
                        ins = v.tensor_tensor(lo[to, hs, :], view3(bank[own, :], 2), hi[own, hs, :].bitcast(F32),
                                              ALU.subtract)
                    ins.then_inc(free, 1)
                elif name == "smax":
                    filled(v, s)
                    p, ic = i // 2, i % 2
                    if u >= 2:
                        filled(v, ("mT", u - 2, p // 4))
                    v.tensor_reduce(negm[u % 2][:, ic, p // 4, p % 4:p % 4 + 5:4], view3(bank[:, :], 2), AX.X, ALU.max,
                                    negate=True).then_inc(free, 1)
                elif name == "v":
                    if u < 8 and i % 2 == 1:
                        filled(v, s)
                        if u >= 1:
                            v.wait_ge(u_ready, u_index(u - 1, 4 * (i // 2) + 3) + 1)
                        v.tensor_copy(V[:, i % 2, 512 * (i // 2):512 * (i // 2) + 512], bank[:, :]).then_inc(free, 1)
                elif name == "rcp":
                    v.wait_ge(p_used, 4 * (u + 1))
                    if u >= 1:
                        v.wait_ge(r_put, 64 * u)
                    v.reciprocal(Rc[:, :], LB[:, 0:T]).then_inc(r_done, 1)
                elif name == "wo":
                    filled(v, s)
                    b = u % 4
                    v.wait_ge(xb_done, order[("xh", [0, 1, 3, 4][u // 4], b)] + 1)
                    v.tensor_tensor(x[:, 2 * b:2 * b + 2, :], view3(bank[:, 0:T], 2), x[:, 2 * b:2 * b + 2, :],
                                    ALU.add).then_inc(free, 1)
                elif name == "ff2":
                    filled(v, s)
                    b = u % 4
                    v.wait_ge(xb_done, order[("xh", 2 + 3 * (u // 4), b)] + 1)
                    v.tensor_tensor(x[:, 2 * b:2 * b + 2, :], view3(bank[:, 0:T], 2), x[:, 2 * b:2 * b + 2, :],
                                    ALU.add).then_inc(free, 1)
                elif name == "ln":
                    if u == 0:
                        v.wait_ge(x_in_sem, 16) if i == 0 else v.wait_ge(misc_in, 32)
                    elif u == 3:
                        emptied(v, ("ff2", i, 0))
                    else:
                        emptied(v, ("wo", {1: 0, 2: 4, 4: 8, 5: 12}[u] + i, 0))
                    n = order[s]
                    if n:
                        v.wait_ge(ln_applied, n)
                    for t in range(2):
                        ins = v.bn_stats(bst[:, t, :], x[:, 2 * i + t, :])
                        if t == 1:
                            link(ins)
                    v.bn_aggr(mv[:, 0, :], bst[:, 0, :])
                    v.bn_aggr(mv[:, 1, :], bst[:, 1, :]).then_inc(ln_stats, 1)
                elif name == "xh":
                    n = order[s]
                    v.wait_ge(ln_stats, n + 1)
                    v.wait_ge(ln_rstd, n + 1)
                    if n:
                        filled(v, hT_steps[n - 1])
                    for t in range(2):
                        ins = v.tensor_scalar(xhat[:, t, :], x[:, 2 * i + t, :], mv[:, t, 0:1], rs[:, t:t + 1],
                                              ALU.subtract, ALU.mult)
                    ins.then_inc(ln_applied, 1)
                elif name == "hT":
                    v.wait_ge(hi_done, hi_count[s])
                    n = order[s]
                    dst = hf1[:, i, :] if u == 3 else hf[:, n % 2, :]
                    if n:
                        v.wait_ge(h_split, n)
                    v.tensor_scalar(dst, bank[:, 0:T], cols[:, 2 * u:2 * u + 1], cols[:, 2 * u + 1:2 * u + 2],
                                    ALU.mult, ALU.add).then_inc(free, 1)
                    emptied(v, s)
                    v.tensor_tensor(hl[:, i, :], dst, hh[:, i, :].bitcast(F32), ALU.subtract).then_inc(h_split, 1)
                elif name == "ff1":
                    v.wait_ge(hi_done, hi_count[s])
                    layer = u // 4
                    if u >= 1:
                        filled(v, ("ff2", u - 1, 0))
                        v.wait_ge(qk_put, 64 * (u if u < NB else 2 * NB))
                    v.scalar_tensor_tensor(gT[:, i, :], bank[:, T:2 * T], cols[:, 12 + 8 * layer + i:13 + 8 * layer + i],
                                           gl[:, i % 2, :], ALU.add, ALU.mult).then_inc(free, 1)
                elif name == "qk":
                    v.wait_ge(hi_done, hi_count[s])
                    if order[s] >= 1:
                        v.wait_ge(qk_put, 64 * order[s])
                    if order[s] < NB:
                        filled(v, ("ff2", order[s], 0))
                    v.tensor_tensor(QKl[:, :], bank[:, :], QKh[:, :].bitcast(F32), ALU.subtract).then_inc(free, 1)
                elif name == "uT":
                    filled(v, s)
                    w = bank[:, :].rearrange("p (h r) -> p h r", r=32)
                    if u > 8:
                        filled(v, ("oT", u - 1, 0))
                    rec = qs[:, 5 + i, :]
                    link(v.reciprocal(rec, w[:, :, DH1]))
                    v.tensor_tensor(on[:, i, :].rearrange("p (h d) -> p h d", d=DH1), w[:, :, 0:DH1],
                                    rec.unsqueeze(2).to_broadcast([D, H, DH1]), ALU.mult).then_inc(free, 1)
                elif name == "qstat":
                    v.wait_ge(loaded[3 + u], 32 if u == 0 else 48)
                    if u == 0:
                        parts = [(slice(0, FULL), L1[:, 0:FULL, :], D), (slice(FULL, 8), L1[0:C, FULL:8, :], C)]
                    else:
                        parts = [(slice(0, 1), F1, D), (slice(1, 2), W2[1][:, :, :], D)]
                    for sl, w, r in parts:
                        ax = AX.XY if (u == 1 and sl.start == 1) else AX.X
                        for o, op, neg in ((0, ALU.max, False), (8, ALU.min, True)):
                            link(v.tensor_reduce(qs[0:r, 0, sl.start + o:sl.stop + o], w, ax, op, negate=neg))
                    v.tensor_copy(qs[:, 7, 8:9], qs[:, 0, 0:1]).then_inc(q_stats, 1)
                elif name == "qscal":
                    v.wait_ge(q_all, u + 1)
                    if u == 1:
                        v.wait_ge(q_quant, 8)
                    mx, mn = qs[:, 1, 0:8], qs[:, 1, 8:16]
                    link(v.tensor_tensor(qs[:, 2, 8:16], mx, mn, ALU.add))
                    link(v.tensor_scalar(qs[:, 2, 0:8], qs[:, 2, 8:16], 1.0 / LEVELS, None, ALU.mult))
                    whole, hi, lo = qs[:, 2, 8:16], qs[:, 5, 0:8], qs[:, 5, 8:16]
                    link(v.tensor_copy(hi.bitcast(F32R), qs[:, 2, 0:8]))
                    link(v.tensor_tensor(lo, qs[:, 2, 0:8], hi, ALU.subtract))
                    link(v.scalar_tensor_tensor(qs[:, 6, 0:8], hi, -LEVELS, whole, ALU.mult, ALU.add))
                    link(v.scalar_tensor_tensor(qs[:, 6, 8:16], lo, -LEVELS, qs[:, 6, 0:8], ALU.mult, ALU.add))
                    link(v.scalar_tensor_tensor(qs[:, 7, 0:8], qs[:, 6, 8:16], 1.0 / LEVELS, qs[:, 2, 0:8],
                                                ALU.mult, ALU.add))
                    link(v.tensor_copy(qs[:, 2, 0:8], qs[:, 7, 0:8]))
                    link(v.reciprocal(qs[:, 8, 0:8], qs[:, 2, 0:8]))
                    link(v.tensor_tensor(qs[:, 3, 8:16], mn, qs[:, 8, 0:8], ALU.mult))
                    link(v.tensor_scalar(qs[:, 4, 8:16], qs[:, 3, 8:16], ROUND, None, ALU.add))
                    link(v.tensor_scalar(qs[:, 3, 0:8], qs[:, 4, 8:16], -ROUND, -1.0, ALU.add, ALU.mult))
                    v.tensor_scalar(qs[:, 4, 0:8], qs[:, 3, 0:8], LEVELS, None, ALU.add).then_inc(q_scal, 1)
                elif name == "qsplit":
                    v.wait_ge(q_quant, 8 if u == 0 else 20)
                    if u == 0:
                        for nm, k in SPLIT.items():
                            j = L1W.index(nm)
                            r = D if j < FULL else C
                            link(v.tensor_copy(L1hi[0:r, k, :], L1[0:r, j, :]))
                            ins = v.tensor_tensor(L1lo[0:r, k, :], L1[0:r, j, :], L1hi[0:r, k, :].bitcast(F32), ALU.subtract)
                    else:
                        link(v.tensor_copy(Wf[1][0][:, :], F1))
                        ins = v.tensor_tensor(Wf[1][1][:, :], F1, Wf[1][0][:, :].bitcast(F32), ALU.subtract)
                    ins.then_inc(q_split, 1)

        @block.tensor
        def _(pe):
            def claim(s):
                k, n = uses[s]
                if n:
                    pe.wait_ge(g_free[k], n)
                elif k == NG:
                    pe.wait_ge(r_done, 8)
                return GB[k]

            def three(dst, w, m, k, start=True, stop=True):
                pe.matmul(dst, w[0], m[0], start=start, stop=False, skip_group_check=True)
                pe.matmul(dst, w[1], m[0], start=False, stop=False, skip_group_check=True)
                return pe.matmul(dst, w[0], m[1], start=False, stop=stop, skip_group_check=True)

            pe.wait_ge(consts, 1)
            for s in plan:
                name, u, i = s
                if name in GENERAL:
                    bank = claim(s)
                    ready = g_ready[uses[s][0]]
                if name in ("q", "k"):
                    a, b = u // 4, u % 4
                    j = 0 if name == "q" else 1
                    of_ctx = a == 1 and name == "k"
                    split_done(pe, ("wsplit", a, j))
                    if of_ctx:
                        pe.wait_ge(c_split, 2)
                        src = [chi[:, b * T:b * T + T], clo[:, b * T:b * T + T]]
                    else:
                        pe.wait_ge(h_split, order[("hT", a, b)] + 1)
                        src = [hh[:, b, :], hl[:, b, :]]
                    rk = C if of_ctx else D
                    for k in range(2):
                        at = D * (2 * i + k)
                        ins = three(bank[:, k * T:k * T + T], [W3[a][z][0:rk, j, at:at + D] for z in range(2)], src, rk)
                    ins.then_inc(ready, 1)
                elif name == "smax":
                    p, ic = i // 2, i % 2
                    if u < 8:
                        emptied(pe, ("q", u, p // 2))
                        emptied(pe, ("k", u, p // 2))
                        pe.wait_ge(k_copied[p // 2], 32 * (u + 1))
                        rk, q_of, k_of = D, Q1, K1
                    else:
                        wait_stacked(pe, u, p // 4)
                        if u in (8, 9):
                            pe.wait_ge(padded[p // 4 if u == 8 else 2], 32)
                        rk, q_of, k_of = C, QS[u % 2], KS[u % 2]
                    for j in range(2):
                        h = 2 * p + j
                        ins = pe.matmul(bank[:, j * T:j * T + T], q_of[0:rk, h, ic * D:ic * D + D], k_of[0:rk, h, :],
                                        start=True, stop=True)
                    ins.then_inc(ready, 1)
                elif name == "mT":
                    emptied(pe, ("smax", u, 8 * i + 7))
                    for ic in range(2):
                        ins = pe.transpose(bank[0:8, ic * D:ic * D + D], negm[u % 2][:, ic, i, :], ident[:, :])
                    ins.then_inc(ready, 1)
                elif name == "v":
                    b = u % 4
                    if u < 8:
                        a, dk, half, jc = u // 4, kdim(u // 4), i // 2, i % 2
                        split_done(pe, ("wsplit", a, 2))
                        at = b * T + jc * D
                        if a == 0:
                            pe.wait_ge(h_split, order[("hT", 0, b)] + 1)
                            keys = [w[:, b, jc * D:jc * D + D] for w in (hh, hl)]
                        else:
                            pe.wait_ge(c_split, 2)
                            keys = [chi[:, at:at + D], clo[:, at:at + D]]
                        w = [W3[a][k][0:dk, 2, 512 * half:512 * half + 512] for k in range(2)]
                        ins = three(bank[:, :], keys, w, dk)
                    else:
                        pe.wait_ge(q_quant, 8)
                        j = L1W.index("v1" if u < 12 else "v2")
                        if u < 12:
                            pe.wait_ge(h_split, order[("hT", 3, b)] + 1)
                        else:
                            pe.wait_ge(loaded[4], 48)
                        for jc in range(2):
                            at = b * T + jc * D
                            keys = hf1[:, b, jc * D:jc * D + D] if u < 12 else cf[:, at:at + D]
                            ins = pe.matmul(bank[:, jc * D:jc * D + D], keys, L1[0:D if u < 12 else C, j, :],
                                            start=True, stop=True)
                    ins.then_inc(ready, 1)
                elif name == "st":
                    n, p, jc = order[s], i // 2, i % 2
                    if n >= NS:
                        pe.wait_ge(exp_done, n - NS + 1)
                    pe.wait_ge(m_row[p // 4], 32 * (u + 1))
                    bank = SB[n % NS]
                    if u < 8:
                        pe.wait_ge(k_padded, 2)
                        pe.wait_ge(q_padded, 1)
                        emptied(pe, ("q", u, p // 2))
                        emptied(pe, ("k", u, p // 2))
                        pe.wait_ge(k_copied[p // 2], 32 * (u + 1))
                        pe.wait_ge(q_copied[p // 2], 32 * (u + 1))
                        terms = [(K1, Q1, D), (K2, Q2, D)]
                    else:
                        terms = [(KS[u % 2], QS[u % 2], C + 1)]
                    for j in range(2):
                        h = 2 * p + j
                        for k, (k_of, q_of, rk) in enumerate(terms):
                            ins = pe.matmul(bank[:, j * T:j * T + T], k_of[0:rk, h, jc * D:jc * D + D], q_of[0:rk, h, :],
                                            start=(k == 0), stop=(k == len(terms) - 1))
                    ins.then_inc(st_done, 1)
                elif name == "pv":
                    n = u_index(u, i)
                    bank = UB
                    if n:
                        pe.wait_ge(u_free, n)
                    pe.wait_ge(exp_done, order[("st", u, 2 * i + 1)] + 1)
                    if u < 8:
                        emptied(pe, ("v", u, 2 * (i // 4)))
                        emptied(pe, ("v", u, 2 * (i // 4) + 1))
                        for jc in range(2):
                            pr = Pr[order[("st", u, 2 * i + jc)] % NP]
                            for j in range(2):
                                h = 2 * i + j
                                ins = pe.matmul(bank[64 * j:64 * j + 64, 0:T], V[:, jc, DH0 * h:DH0 * h + DH0],
                                                pr[:, j * T:j * T + T], start=(jc == 0), stop=(jc == 1))
                    else:
                        emptied(pe, ("v", u, 0))
                        pe.wait_ge(zeroed, 1 if u == 8 else 2)
                        for jc in range(2):
                            for c in range(4):
                                h = 4 * (i // 2) + c
                                pr = Pr[order[("st", u, 2 * (h // 2) + jc)] % NP]
                                ins = pe.matmul(bank[32 * c:32 * c + 32, 0:T], V1[u % 2][:, jc, h, :],
                                                pr[:, (h % 2) * T:(h % 2) * T + T], start=(jc == 0), stop=(jc == 1),
                                                tile_position=(0, 32 * c))
                    ins.then_inc(u_ready, 1)
                elif name == "L":
                    k = i // 2
                    if k == 0 and u >= 1:
                        pe.wait_ge(r_done, u)
                    for jc in range(2):
                        for c in range(4):
                            h = 4 * k + c
                            pr = Pr[order[("st", u, 2 * (h // 2) + jc)] % NP]
                            ins = pe.matmul(LB[32 * c:32 * c + 32, 0:T], lsel[:, k, :], pr[:, (h % 2) * T:(h % 2) * T + T],
                                            start=(k == 0 and jc == 0), stop=(k == 3 and jc == 1),
                                            tile_position=(0, 32 * c))
                    ins.then_inc(p_used, 1)
                elif name == "wo":
                    if u < 8:
                        pe.wait_ge(wo_loaded, 32)
                        pe.wait_ge(norm_done, 2 * (u + 1))
                        for t in range(2):
                            for p in range(PAIRS):
                                ins = pe.matmul(bank[:, t * D:t * D + D], U[:, (8 * u + p) % RING, t * D:t * D + D],
                                                Wo[u // 4][:, p, :], start=(p == 0), stop=(p == PAIRS - 1))
                    else:
                        emptied(pe, ("oT", u, 0))
                        j = L1W.index("o1" if u < 12 else "o2")
                        for t in range(2):
                            ins = pe.matmul(bank[:, t * D:t * D + D], oT[:, t * D:t * D + D], L1[:, j, :],
                                            start=True, stop=True)
                    ins.then_inc(ready, 1)
                elif name == "hT":
                    pe.wait_ge(ln_applied, order[s] + 1)
                    for t in range(2):
                        ins = pe.transpose(bank[:, t * D:t * D + D], xhat[:, t, :], ident[:, :])
                    ins.then_inc(ready, 1)
                elif name == "ff1":
                    layer, b = u // 4, u % 4
                    pe.wait_ge(h_split, order[("hT", 2 + 3 * layer, b)] + 1)
                    if layer == 0:
                        split_done(pe, ("wsplit", 2, 0))
                    else:
                        pe.wait_ge(q_split, 2)
                    for half, ch in ((0, NCH + i), (1, i)):
                        ins = three(bank[:, half * T:half * T + T], [w[:, ch * D:ch * D + D] for w in Wf[layer]],
                                    [hh[:, b, :], hl[:, b, :]], D)
                    ins.then_inc(ready, 1)
                elif name == "ff2":
                    layer = u // 4
                    emptied(pe, ("ff1", u, NCH - 1))
                    if layer == 0:
                        pe.wait_ge(loaded[2], 32)
                    else:
                        pe.wait_ge(q_quant, 20)
                    for t in range(2):
                        for c in range(NCH):
                            ins = pe.matmul(bank[:, t * D:t * D + D], gT[:, c, t * D:t * D + D], W2[layer][:, c, :],
                                            start=(c == 0), stop=(c == NCH - 1))
                    ins.then_inc(ready, 1)
                elif name == "qk":
                    b, cross = u % 4, u >= 12
                    pe.wait_ge(q_split, 1)
                    pe.wait_ge(h_split, order[("hT", 4 if cross else 3, b)] + 1)
                    for half, nm in ((0, "q2" if cross else "q1"), (1, "k2" if cross else "k1")):
                        r = C if nm == "k2" else D
                        k = SPLIT[nm]
                        src = [chi[:, b * T:b * T + T], clo[:, b * T:b * T + T]] if nm == "k2" else [hh[:, b, :], hl[:, b, :]]
                        ins = three(bank[:, half * T:half * T + T], [L1hi[0:r, k, :], L1lo[0:r, k, :]], src, r)
                    ins.then_inc(ready, 1)
                elif name == "uT":
                    pe.wait_ge(u_free, u_end(u))
                    for g4 in range(4):
                        at = (64 + 4 * (u - 8) + g4) % RING
                        ins = pe.transpose(bank[:, g4 * D:g4 * D + D], U[:, at, i * D:i * D + D], ident[:, :])
                    ins.then_inc(ready, 1)
                elif name == "oT":
                    emptied(pe, ("uT", u, 0))
                    emptied(pe, ("uT", u, 1))
                    for t in range(2):
                        ins = pe.transpose(bank[:, t * D:t * D + D], on[:, t, :], ident[:, :])
                    ins.then_inc(ready, 1)


def kernel(**inputs):
    import concourse.bacc as bacc
    from concourse.bass_utils import run_bass_kernel_spmd

    a = {k: np.asarray(v) for k, v in inputs.items()}
    L0, L1n = "L0_xattn_", "L1_xattn_"
    flat = lambda w: np.ascontiguousarray(w)
    by_p = lambda w, n: flat(w.reshape(n, D, -1).transpose(1, 0, 2))
    arrays = {
        "x_tok": by_p(a["x"], 2 * NB),
        "ctx_t": flat(a["ctx_768"].reshape(NB * T, C).T),
        **{f"{w.lower()}{k}": a[f"{L0}{w}{k}"] for w in ("Wq", "Wk", "Wv") for k in (1, 2)},
        "wo1": by_p(a[L0 + "Wo1"], PAIRS), "wo2": by_p(a[L0 + "Wo2"], PAIRS),
        "wp": a[L0 + "Wp"], "w2": by_p(a[L0 + "W2"], NCH),
        "l1_full": flat(np.stack([a[f"{L1n}{n}_w"].T for n in L1W[:FULL]], 1)),
        "l1_ctx": flat(np.stack([a[f"{L1n}{n}_w"].T for n in L1W[FULL:]], 1)),
        "ff1_t": flat(a[L1n + "ff1_w"].T), "ff2_t": by_p(a[L1n + "ff2_w"].T, NCH),
        "cols": flat(np.concatenate([np.stack([
            a[L0 + "g1"], a[L0 + "be1"], a[L0 + "g2"], a[L0 + "be2"], a[L0 + "g3"], a[L0 + "be3"],
            a[L1n + "ln1_g"], a[L1n + "ln1_b"], a[L1n + "ln2_g"], a[L1n + "ln2_b"], a[L1n + "ln3_g"], a[L1n + "ln3_b"],
        ], 1), a[L0 + "bp"].reshape(8, D).T, a[L1n + "ff1_b"].reshape(8, D).T], 1)),
        "rows": flat(np.stack([a[L0 + "bo1"], a[L0 + "bo2"], a[L0 + "b2"],
                               a[L1n + "o1_b"], a[L1n + "o2_b"], a[L1n + "ff2_b"]], 0)),
    }
    nc = bacc.Bacc("TRN2", target_bir_lowering=False, num_devices=1)
    t = {n: nc.dram_tensor("in_" + n, w.shape, F32, kind="ExternalInput").ap() for n, w in arrays.items()}
    out = nc.dram_tensor("out", (D, 2 * NB, D), F32, kind="ExternalOutput").ap()
    build(nc, t["x_tok"], t["ctx_t"], [[t[f"{w}{k}"] for w in ("wq", "wk", "wv")] for k in (1, 2)],
          [t["wo1"], t["wo2"]], t["wp"], t["w2"], (t["l1_full"], t["l1_ctx"]), t["ff1_t"], t["ff2_t"],
          t["cols"], t["rows"], out)
    r = run_bass_kernel_spmd(nc, [{"in_" + n: w for n, w in arrays.items()}], core_ids=[0])
    got = r.results[0]["out"]
    return flat(got.transpose(1, 0, 2)).reshape(NB, T, D)
```
